# Optimizing a Trainium2 kernel written in Bass

```python
import numpy as np
import jax
import jax.numpy as jnp

def _softmax(x, axis=-1):
    return jax.nn.softmax(x, axis=axis)

def _gelu(x):
    return jax.nn.gelu(x, approximate=True)

def _silu(x):
    return jax.nn.silu(x)

def _sigmoid(x):
    return jax.nn.sigmoid(x)

def _layernorm(x, axis=-1, eps=1e-05):
    m = jnp.mean(x, axis=axis, keepdims=True)
    v = jnp.var(x, axis=axis, keepdims=True)
    return (x - m) / jnp.sqrt(v + eps)

def _scatter_add(tgt, idx, src, axis=0):
    return tgt.at[idx].add(src)

def _segment_sum(src, seg, n):
    return jax.ops.segment_sum(src, seg, n)
kernel_name = 'mk_adj_ffn_d1_adj_r2_523c96'

def setup_inputs(seed: int=0):
    np.random.seed(seed)
    _w = jnp.asarray

    def _rec_inputs():
        import jax
        import jax.numpy as jnp
        _gk = jax.random.key(seed)
        x = 7.22e-05 + 1 * jax.random.normal(jax.random.fold_in(_gk, 1), (4096, 512), jnp.float32)
        _a = jax.random.bernoulli(jax.random.fold_in(_gk, 2), 0.00195312, (4096, 4096))
        _a = jnp.logical_or(_a, jnp.swapaxes(_a, -1, -2))
        _a = jnp.logical_or(_a, jnp.eye(4096, dtype=bool))
        _af = _a.astype(jnp.float32)
        adj = _af
        return (x, adj)
    x, adj = _rec_inputs()

    def _L0_gnn_setup():
        import jax, jax.numpy as jnp
        import numpy as np
        N = 4096
        D = 512
        key = jax.random.key(seed)
        ks = jax.random.split(key, 13)
        w_scale = 1.0 / np.sqrt(D)
        inp = {'query': jax.random.normal(ks[0], (N, D), dtype=jnp.float32), 'key': jax.random.normal(ks[1], (N, D), dtype=jnp.float32), 'value': jax.random.normal(ks[2], (N, D), dtype=jnp.float32), 'adj_matrix': jax.random.randint(ks[3], (N, N), 0, 2).astype(jnp.float32), 'Wq': jax.random.normal(ks[4], (D, D), dtype=jnp.float32) * w_scale, 'bq': jax.random.normal(ks[5], (D,), dtype=jnp.float32) * 0.01, 'Wk': jax.random.normal(ks[6], (D, D), dtype=jnp.float32) * w_scale, 'bk': jax.random.normal(ks[7], (D,), dtype=jnp.float32) * 0.01, 'Wv': jax.random.normal(ks[8], (D, D), dtype=jnp.float32) * w_scale, 'bv': jax.random.normal(ks[9], (D,), dtype=jnp.float32) * 0.01, 'Wm': jax.random.normal(ks[10], (D, D), dtype=jnp.float32) * w_scale, 'bm': jax.random.normal(ks[11], (D,), dtype=jnp.float32) * 0.01}
        return inp
    _L0_gnn_all = _L0_gnn_setup()
    _L0_gnn_in = {k: v for k, v in _L0_gnn_all.items() if k in ('key', 'value', 'Wq', 'bq', 'Wk', 'bk', 'Wv', 'bv', 'Wm', 'bm')}
    del _L0_gnn_all

    def _L0_ffn_setup():
        import jax, jax.numpy as jnp
        import numpy as np
        IN_DIM = 512
        OUT_DIM = 512
        NUM_EXPERTS = 8
        TOP_K = 2
        key = jax.random.key(seed)
        ks = jax.random.split(key, 5)
        s = 1.0 / np.sqrt(IN_DIM)
        x = jax.random.normal(ks[0], (4, 1024, IN_DIM), dtype=jnp.float32)
        Wg = jax.random.uniform(ks[1], (IN_DIM, NUM_EXPERTS), jnp.float32, -s, s)
        bg = jnp.zeros((NUM_EXPERTS,), jnp.float32)
        We = jax.random.uniform(ks[2], (NUM_EXPERTS, OUT_DIM, IN_DIM), jnp.float32, -s, s)
        be = jax.random.uniform(ks[3], (NUM_EXPERTS, OUT_DIM), jnp.float32, -s, s)
        return {'x': x, 'Wg': Wg, 'bg': bg, 'We': We, 'be': be}
    _L0_ffn_all = _L0_ffn_setup()
    _L0_ffn_in = {k: v for k, v in _L0_ffn_all.items() if k in ('Wg', 'bg', 'We', 'be')}
    del _L0_ffn_all
    return {'x': x, 'adj': adj, 'L0_gnn_key': _L0_gnn_in['key'], 'L0_gnn_value': _L0_gnn_in['value'], 'L0_gnn_Wq': _L0_gnn_in['Wq'], 'L0_gnn_bq': _L0_gnn_in['bq'], 'L0_gnn_Wk': _L0_gnn_in['Wk'], 'L0_gnn_bk': _L0_gnn_in['bk'], 'L0_gnn_Wv': _L0_gnn_in['Wv'], 'L0_gnn_bv': _L0_gnn_in['bv'], 'L0_gnn_Wm': _L0_gnn_in['Wm'], 'L0_gnn_bm': _L0_gnn_in['bm'], 'L0_ffn_Wg': _L0_ffn_in['Wg'], 'L0_ffn_bg': _L0_ffn_in['bg'], 'L0_ffn_We': _L0_ffn_in['We'], 'L0_ffn_be': _L0_ffn_in['be']}

def reference(x, adj, L0_gnn_key, L0_gnn_value, L0_gnn_Wq, L0_gnn_bq, L0_gnn_Wk, L0_gnn_bk, L0_gnn_Wv, L0_gnn_bv, L0_gnn_Wm, L0_gnn_bm, L0_ffn_Wg, L0_ffn_bg, L0_ffn_We, L0_ffn_be):
    import jax
    import jax.numpy as jnp

    def _L0_gnn_ref(query, key, value, adj_matrix, Wq, bq, Wk, bk, Wv, bv, Wm, bm):
        import jax, jax.numpy as jnp
        import numpy as np
        N = 4096
        D = 512
        q = query @ Wq.T + bq
        k = key @ Wk.T + bk
        v = value @ Wv.T + bv
        scale = q.shape[0] ** 0.5
        scores = jnp.einsum('nd,md->nm', q, k) / scale
        adj_scores = scores * adj_matrix
        adj_scores = jnp.where(jnp.abs(adj_scores) < 1e-05, -1000000000.0, adj_scores)
        prob = jax.nn.softmax(adj_scores, axis=-1)
        x = jnp.einsum('nm,md->nd', prob, v)
        return x @ Wm.T + bm

    def _L0_ffn_ref(x, Wg, bg, We, be):
        import jax, jax.numpy as jnp
        import numpy as np
        IN_DIM = 512
        OUT_DIM = 512
        NUM_EXPERTS = 8
        TOP_K = 2
        gate = jax.nn.softmax(x @ Wg + bg, axis=-1)
        topk_vals, topk_idx = jax.lax.top_k(gate, TOP_K)
        onehot = jax.nn.one_hot(topk_idx, NUM_EXPERTS, dtype=gate.dtype)
        gate_sparse = jnp.einsum('bsk,bske->bse', topk_vals, onehot)
        gate_sparse = gate_sparse / jnp.sum(gate_sparse, axis=-1, keepdims=True)
        y = jnp.einsum('bsi,eoi->bseo', x, We) + be[None, None, :, :].transpose(0, 1, 2, 3)
        out = jnp.einsum('bseo,bse->bso', y, gate_sparse)
        return out
    x = x + _L0_gnn_ref(_layernorm(x, axis=-1), L0_gnn_key, L0_gnn_value, adj, L0_gnn_Wq, L0_gnn_bq, L0_gnn_Wk, L0_gnn_bk, L0_gnn_Wv, L0_gnn_bv, L0_gnn_Wm, L0_gnn_bm)
    x = x + _L0_ffn_ref(_layernorm(x, axis=-1)[None], L0_ffn_Wg, L0_ffn_bg, L0_ffn_We, L0_ffn_be)[0]
    return x

_drawn_inputs = setup_inputs


def setup_inputs(seed=0):
    import zlib

    import numpy as np

    out = dict(_drawn_inputs(seed))
    spreads = {'L0_ffn_bg': (0.0, 0.1)}
    factors = {'L0_gnn_bq': 8.0, 'L0_gnn_bk': 8.0, 'L0_ffn_be': 3.43}
    for name, (base, spread) in spreads.items():
        noise = np.random.default_rng([zlib.crc32(name.encode()), seed]).standard_normal(out[name].shape)
        drawn = base * np.exp(spread * noise) if base else spread * noise
        out[name] = jnp.asarray(drawn.astype(out[name].dtype))
    for name, factor in factors.items():
        out[name] = (out[name] * factor).astype(out[name].dtype)
    return out
```

```python
from contextlib import ExitStack

import concourse.bass as bass
from concourse import mybir

F32 = mybir.dt.float32
F16 = mybir.dt.float16
U32 = mybir.dt.uint32
ALU = mybir.AluOpType
ACT = mybir.ActivationFunctionType
AX_X = mybir.AxisListType.X

P = 128
NEG = -1e9
THRESHOLD = 1e-5
EPS = 1e-5
WS = 16.0


def graph_attention_moe_kernel(nc, x, adj, keyT, valueT, Wq, bq, Wk, bk, Wv, bv, WmT, bm, Wg, bg, WeT, be, out):
    N, D = x.shape
    E = WeT.shape[0]
    KC = D // P
    T = N // P
    GT = D // P
    G = T // GT
    GW = GT * P
    CW = 512
    C = N // CW
    MT = CW // P
    SS = WS * float(N) ** 0.5
    assert D == 512 and GW == 512 and SS == 1024.0

    ctx = ExitStack()
    with ctx:
        def sb(name, shape, dt):
            return ctx.enter_context(nc.sbuf_tensor(name, shape, dt))

        def sem(name):
            return ctx.enter_context(nc.semaphore(name))

        key_region = sb("key_region", [P, 2 * KC * N], F16)
        val_region = sb("val_region", [P, 2 * T * D], F16)
        work = sb("work", [P, 17408], F32)

        kT = key_region[:, :].rearrange("p (h k n) -> p h k n", h=2, k=KC)
        v = val_region[:, :].rearrange("p (h t d) -> p h t d", h=2, t=T)
        we = key_region[:, :].rearrange("p (h e k o) -> p h e k o", h=2, e=E, k=KC)
        raw = val_region[:, 0:8 * KC * D].bitcast(F32).rearrange("p (w k d) -> p w k d", w=4, k=KC)
        wq_raw, wk_raw, wv_raw, wmT_raw = (raw[:, i] for i in range(4))

        taken = [0]

        def carve(words):
            at = taken[0]
            taken[0] += words
            assert taken[0] <= 17408, taken
            return work[:, at:at + words]

        foldA = carve(KC * D).bitcast(F16).rearrange("p (h k d) -> p h k d", h=2, k=KC)
        foldV = carve(KC * D).bitcast(F16).rearrange("p (h k d) -> p h k d", h=2, k=KC)
        g_row = carve(D)
        key_in = carve(KC * GW).rearrange("p (k n) -> p k n", k=KC)
        val_in = carve(KC * GW).rearrange("p (k n) -> p k n", k=KC)
        x_in = carve(GT * D).rearrange("p (t d) -> p t d", t=GT)
        vT = carve(KC * GW).bitcast(F16).rearrange("p (h k n) -> p h k n", h=2, k=KC)
        xnT = carve(KC * GW).bitcast(F16).rearrange("p (h k n) -> p h k n", h=2, k=KC)
        q_out = carve(KC * GW).bitcast(F16).rearrange("p (t h k n) -> p t h k n", t=GT, h=2, k=KC)
        r_junk = carve(D)
        x_wide = [q_out.rearrange("p t h k n -> p (t h k n)").bitcast(F32)[:, i * D:(i + 1) * D]
                  .rearrange("p (k n) -> p k n", k=KC) for i in range(2)]
        taken[0] = 0
        w = carve(N)
        prob = carve(N)
        adj_in = carve(N).rearrange("p (c n) -> p c n", c=C)
        s_adj = carve(2 * CW).rearrange("p (b n) -> p b n", b=2)
        s_abs = carve(2 * CW).rearrange("p (b n) -> p b n", b=2)
        pT = carve(2 * MT * P).bitcast(F16).rearrange("p (b h m n) -> p b h m n", b=2, h=2, m=MT)
        q_in = carve(KC * P).bitcast(F16).rearrange("p (h k n) -> p h k n", h=2, k=KC)
        x_res = carve(D)
        x1_out = carve(D)
        taken[0] = 0
        we_in = carve(2 * KC * D).rearrange("p (b k o) -> p b k o", b=2, k=KC)
        y_in = carve(2 * D).rearrange("p (b d) -> p b d", b=2)
        yn = carve(D)
        ynT = carve(2 * KC * P).bitcast(F16).rearrange("p (b h k n) -> p b h k n", b=2, h=2, k=KC)
        ynT32 = carve(KC * P).rearrange("p (k n) -> p k n", k=KC)
        acc = carve(2 * D).rearrange("p (b d) -> p b d", b=2)

        ident = sb("ident", [P, P], F32)
        ones = sb("ones", [P, P], F32)
        neg_half = sb("neg_half", [P, GT], F32)
        c_row = sb("c_row", [P, D], F32)
        bq_col = sb("bq_col", [P, KC], F32)
        bk_col = sb("bk_col", [P, KC], F32)
        bv_col = sb("bv_col", [P, KC], F32)
        bm_row = sb("bm_row", [1, D], F32)
        bg_row = sb("bg_row", [1, E], F32)
        be_in = sb("be_in", [E, D], F32)
        wg = sb("wg", [P, KC, E], F32)
        u_col = sb("u_col", [P, KC], F32)
        c0 = sb("c0", [P, 1], F32)
        r_tmp = sb("r_tmp", [P, GT], F32)
        r_all = sb("r_all", [P, T], F32)
        r_cur = sb("r_cur", [P, 1], F32)
        stats = sb("stats", [P, GT, 6], F32)
        moments = sb("moments", [P, GT, 2], F32)
        var_eps = sb("var_eps", [P, GT], F32)
        rstd = sb("rstd", [P, GT], F32)
        max_part = sb("max_part", [P, C], F32)
        row_max = sb("row_max", [P, 1], F32)
        exp_bias = sb("exp_bias", [P, 1], F32)
        sum_part = sb("sum_part", [P, C], F32)
        row_sum = sb("row_sum", [P, 1], F32)
        row_sum_ws = sb("row_sum_ws", [P, 1], F32)
        inv_sum = sb("inv_sum", [P, 1], F32)
        iota_e = sb("iota_e", [P, E], F32)
        logits = sb("logits", [P, E], F32)
        top8 = sb("top8", [P, 8], F32)
        top_idx = sb("top_idx", [P, 8], U32)
        top_idx_f = sb("top_idx_f", [P, 8], F32)
        gap = sb("gap", [P, 1], F32)
        egap = sb("egap", [P, 1], F32)
        den = sb("den", [P, 1], F32)
        gate = sb("gate", [P, 2], F32)
        gate_1 = sb("gate_1", [P, E], F32)
        gate_2 = sb("gate_2", [P, E], F32)
        gates = sb("gates", [P, E], F32)
        gates_ws = sb("gates_ws", [P, 2, E], F32)
        gatesT = sb("gatesT", [E, P], F32)

        ps = ctx.enter_context(nc.psum_tensor("ps", [P, 8, 512], F32))
        tr_bank = lambda i: ps[:, i % 4, :]
        mm_bank = lambda i: ps[:, 4 + i % 4, :]
        s_bank = lambda c: ps[:, c % 2, :]
        pT_bank = lambda c: ps[:, 2 + c % 2, :]
        o_bank = ps[:, 4, :]
        y_bank = lambda e: ps[:, e % 4, :]
        ynT_bank = ps[:, 5, :]
        gate_bank = ps[:, 6, 0:E]
        gateT_bank = ps[0:E, 6, 128:256]
        bias_bank = ps[:, 7, :]

        q_dram = nc.dram_tensor("q_scratch", (T, P, 2 * KC * P), F16, kind="Internal").ap()
        x1_dram = nc.dram_tensor("x1_scratch", (T, P, D), F32, kind="Internal").ap()
        x_tiles = x.rearrange("(t p) d -> t p d", p=P)
        x_groups = x.rearrange("(t p) d -> p t d", p=P)
        keyT_v = keyT.rearrange("(k p) n -> p k n", p=P)
        valueT_v = valueT.rearrange("(k p) n -> p k n", p=P)
        adj_tiles = adj.rearrange("(t p) n -> t p n", p=P)
        out_tiles = out.rearrange("(t p) d -> t p d", p=P)
        weT_v = WeT.rearrange("e (k p) o -> e p k o", p=P)

        w_loaded = sem("w_loaded")
        b_loaded = sem("b_loaded")
        consts_ready = sem("consts_ready")
        ident_step = sem("ident_step")
        ones_ready = sem("ones_ready")
        wait_passed = sem("wait_passed")
        bias_cols_wide = sem("bias_cols_wide")
        fold_mm = sem("fold_mm")
        fold_hi = sem("fold_hi")
        fold_out = sem("fold_out")
        key_loaded = sem("key_loaded")
        key_hi = sem("key_hi")
        key_lo = sem("key_lo")
        val_loaded = sem("val_loaded")
        val_hi = sem("val_hi")
        val_lo = sem("val_lo")
        x_loaded = sem("x_loaded")
        stats_done = sem("stats_done")
        moments_done = sem("moments_done")
        var_done = sem("var_done")
        rstd_done = sem("rstd_done")
        xn_done = sem("xn_done")
        r_done = sem("r_done")
        r_kept = sem("r_kept")
        xnT_mm = sem("xnT_mm")
        xnT_hi = sem("xnT_hi")
        xnT_lo = sem("xnT_lo")
        proj_mm = sem("proj_mm")
        proj_hi = sem("proj_hi")
        proj_lo = sem("proj_lo")
        q_stored = sem("q_stored")
        q_loaded = sem("q_loaded")
        adj_loaded = [sem(f"adj_loaded{c}") for c in range(C)]
        xres_loaded = sem("xres_loaded")
        rcur_done = sem("rcur_done")
        s_mm = sem("s_mm")
        s_read = sem("s_read")
        abs_done = sem("abs_done")
        mask_done = sem("mask_done")
        w_done = sem("w_done")
        max_done = sem("max_done")
        bias_done = sem("bias_done")
        exp_done = sem("exp_done")
        pT_mm = sem("pT_mm")
        pT_hi = sem("pT_hi")
        pT_lo = sem("pT_lo")
        pv_mm = sem("pv_mm")
        sum_done = sem("sum_done")
        sum_ws_done = sem("sum_ws_done")
        inv_done = sem("inv_done")
        xc_done = sem("xc_done")
        x1_done = sem("x1_done")
        x1_stored = sem("x1_stored")
        we_loaded = [sem(f"we_loaded{b}") for b in range(2)]
        we_hi = sem("we_hi")
        we_lo = sem("we_lo")
        y_loaded = [sem(f"y_loaded{b}") for b in range(2)]
        ystats_done = sem("ystats_done")
        ymom_done = sem("ymom_done")
        yvar_done = sem("yvar_done")
        yrstd_done = sem("yrstd_done")
        yn_done = sem("yn_done")
        ynT_mm = sem("ynT_mm")
        ynT_act = sem("ynT_act")
        ynT_lo = sem("ynT_lo")
        gate_mm = sem("gate_mm")
        gate_step = sem("gate_step")
        egap_done = sem("egap_done")
        gates_done = sem("gates_done")
        gateT_mm = sem("gateT_mm")
        gateT_out = sem("gateT_out")
        bias_mm = sem("bias_mm")
        acc_start = sem("acc_start")
        y_mm = sem("y_mm")
        y_added = sem("y_added")
        out_stored = [sem(f"out_stored{b}") for b in range(2)]

        is0 = lambda g: isinstance(g, int) and g == 0
        isl = lambda g, n: isinstance(g, int) and g == n - 1

        block = ctx.enter_context(nc.Block())

        @block.sync
        def _(sp):
            with nc.allow_non_contiguous_dma(reason="small bias columns"):
                for col, src in ((bq_col, bq), (bk_col, bk), (bv_col, bv)):
                    sp.dma_start(col[:, :], src.rearrange("(k p) -> p k", p=P)).then_inc(b_loaded, 16)
                sp.dma_start(wg[:, :, :], Wg.rearrange("(k p) e -> p k e", p=P)).then_inc(b_loaded, 16)
            sp.dma_start(bm_row[:, :], bm.rearrange("(a d) -> a d", a=1)).then_inc(b_loaded, 16)
            sp.dma_start(bg_row[:, :], bg.rearrange("(a d) -> a d", a=1)).then_inc(b_loaded, 16)
            sp.dma_start(be_in[:, :], be).then_inc(b_loaded, 16)
            for dst, src in ((wq_raw, Wq), (wk_raw, Wk), (wv_raw, Wv), (wmT_raw, WmT)):
                sp.dma_start(dst, src.rearrange("(k p) d -> p k d", p=P)).then_inc(w_loaded, 16)

            def load_group(g):
                sp.dma_start(val_in, valueT_v[:, :, bass.ds(g * GW, GW)]).then_inc(val_loaded, 16)
                sp.dma_start(x_in, x_groups[:, bass.ds(g * GT, GT), :]).then_inc(x_loaded, 16)
                sp.dma_start(key_in, keyT_v[:, :, bass.ds(g * GW, GW)]).then_inc(key_loaded, 16)

            load_group(0)
            with sp.Fori(0, G - 1) as g:
                sp.wait_ge(val_lo, g + 1)
                sp.dma_start(val_in, valueT_v[:, :, bass.ds(g * GW + GW, GW)]).then_inc(val_loaded, 16)
                sp.wait_ge(xnT_mm, g * GT + GT)
                sp.wait_ge(r_done, g * GT + GT)
                sp.dma_start(x_in, x_groups[:, bass.ds(g * GT + GT, GT), :]).then_inc(x_loaded, 16)
                sp.wait_ge(key_lo, g + 1)
                sp.dma_start(key_in, keyT_v[:, :, bass.ds(g * GW + GW, GW)]).then_inc(key_loaded, 16)
                sp.wait_ge(proj_lo, g * 8 + 8)
                sp.dma_start(q_dram[bass.ds(g * GT, GT)].rearrange("t p f -> p t f"),
                             q_out.rearrange("p t h k n -> p t (h k n)")).then_inc(q_stored, 16)
            sp.wait_ge(proj_lo, G * 8)
            sp.dma_start(q_dram[T - GT:T].rearrange("t p f -> p t f"),
                         q_out.rearrange("p t h k n -> p t (h k n)")).then_inc(q_stored, 16)

            sp.wait_ge(r_kept, G)
            sp.wait_ge(proj_mm, G * 8)
            sp.wait_ge(q_stored, 16 * G)
            sp.dma_start(q_in, q_dram[0]).then_inc(q_loaded, 16)
            for c in range(C):
                sp.dma_start(adj_in[:, c, :], adj_tiles[0, :, c * CW:(c + 1) * CW]).then_inc(adj_loaded[c], 16)
            sp.dma_start(x_res, x_tiles[0]).then_inc(xres_loaded, 16)

            def residual_io(t):
                sp.wait_ge(x1_done, t + 1)
                sp.dma_start(x_res, x_tiles[t + 1]).then_inc(xres_loaded, 16)
                sp.dma_start(x1_dram[t], x1_out).then_inc(x1_stored, 16)

            def attend_io(t):
                for c in range(C):
                    sp.wait_ge(s_read, t * C - C + c + 1)
                    sp.dma_start(adj_in[:, c, :], adj_tiles[t, :, c * CW:(c + 1) * CW]).then_inc(adj_loaded[c], 16)
                sp.wait_ge(s_mm, t * C)
                sp.dma_start(q_in, q_dram[t]).then_inc(q_loaded, 16)

            attend_io(1)
            with sp.Fori(2, T) as t:
                attend_io(t)
                residual_io(t - 2)
            residual_io(T - 2)
            sp.wait_ge(exp_done, T * C)
            for e in range(2):
                sp.dma_start(we_in[:, e], weT_v[e]).then_inc(we_loaded[e], 16)
            sp.wait_ge(x1_done, T)
            sp.dma_start(x1_dram[T - 1], x1_out).then_inc(x1_stored, 16)
            sp.wait_ge(pT_mm, T * C)
            sp.wait_ge(x1_stored, 16 * T)
            for b in range(2):
                sp.dma_start(y_in[:, b], x1_dram[b]).then_inc(y_loaded[b], 16)
            for e in range(2, E):
                sp.wait_ge(we_lo, e - 1)
                sp.dma_start(we_in[:, e % 2], weT_v[e]).then_inc(we_loaded[e % 2], 16)

            def expert_io(t, b, last):
                if not last:
                    sp.wait_ge(acc_start, t + 1)
                    sp.dma_start(y_in[:, b], x1_dram[t + 2]).then_inc(y_loaded[b], 16)
                sp.wait_ge(y_added, t * E + E)
                sp.dma_start(out_tiles[t], acc[:, b]).then_inc(out_stored[b], 16)

            with sp.Fori(0, T // 2 - 1) as i:
                expert_io(i * 2, 0, False)
                expert_io(i * 2 + 1, 1, False)
            expert_io(T - 2, 0, True)
            expert_io(T - 1, 1, True)
            for b in range(2):
                sp.wait_ge(out_stored[b], 16 * (T // 2))

        @block.gpsimd
        def _(pool):
            nc.gpsimd.memset(ident[:, :], 0.0).then_inc(ident_step, 1)
            pool.wait_ge(ident_step, 1)
            nc.gpsimd.affine_select(out=ident[:, :], in_=ident[:, :], compare_op=ALU.not_equal, fill=1.0, base=0,
                                    pattern=[[-1, P]], channel_multiplier=1).then_inc(consts_ready, 1)
            for e in range(E):
                last = nc.gpsimd.memset(iota_e[:, e:e + 1], float(e))
            last.then_inc(consts_ready, 1)
            nc.gpsimd.memset(neg_half[:, :], -0.5).then_inc(ident_step, 1)
            pool.wait_ge(ident_step, 2)
            with pool.Fori(0, G) as g:
                pool.wait_ge(var_done, g + 1)
                nc.gpsimd.tensor_tensor(rstd[:, :], var_eps[:, :], neg_half[:, :], ALU.pow).then_inc(rstd_done, 1)
            with pool.Fori(0, T) as t:
                pool.wait_ge(yvar_done, t + 1)
                nc.gpsimd.tensor_tensor(rstd[:, 0:1], var_eps[:, 0:1], neg_half[:, 0:1], ALU.pow).then_inc(yrstd_done, 1)

        @block.scalar
        def _(act):
            for i in range(2 * KC):
                act.wait_ge(fold_mm, i + 1)
                dst = (foldA if i < KC else foldV)[:, 0, i % KC, :]
                nc.scalar.activation(dst, ps[:, i, :], ACT.Copy, scale=WS).then_inc(fold_hi, 1)

            def split_values(g):
                act.wait_ge(val_loaded, g * 16 + 16)
                if not is0(g):
                    act.wait_ge(proj_mm, g * 8 - 4)
                nc.scalar.activation(vT[:, 0], val_in, ACT.Copy).then_inc(val_hi, 1)

            def project(g, last=False):
                for s in range(GT):
                    act.wait_ge(xnT_mm, g * GT + s + 1)
                    if s == 0 and not is0(g):
                        act.wait_ge(proj_mm, g * 8)
                    nc.scalar.activation(xnT[:, 0, :, s * P:(s + 1) * P],
                                         tr_bank(s).rearrange("p (k n) -> p k n", k=KC), ACT.Copy).then_inc(xnT_hi, 1)
                    act.wait_ge(proj_mm, g * 8 + s + 1)
                    nc.scalar.activation(v[:, 0, g * GT + s, :], mm_bank(s), ACT.Copy).then_inc(proj_hi, 1)
                act.wait_ge(key_loaded, g * 16 + 16)
                nc.scalar.activation(kT[:, 0, :, bass.ds(g * GW, GW)], key_in, ACT.Copy).then_inc(key_hi, 1)
                if not last:
                    split_values(g + 1)
                for j in range(KC):
                    act.wait_ge(proj_mm, g * 8 + 4 + j + 1)
                    if j == 0 and not is0(g):
                        act.wait_ge(q_stored, g * 16)
                    nc.scalar.activation(q_out[:, :, 0, j, :], mm_bank(j).rearrange("p (t n) -> p t n", t=GT),
                                         ACT.Identity, bias=u_col[:, j:j + 1]).then_inc(proj_hi, 1)

            act.wait_ge(fold_out, 2 * KC + 3)
            split_values(0)
            project(0)
            with act.Fori(1, G - 1) as g:
                project(g)
            project(G - 1, last=True)

            def absolute(t, c):
                act.wait_ge(s_read, t * C + c + 1)
                if not (is0(t) and c < 2):
                    act.wait_ge(w_done, t * C + c - 1)
                nc.scalar.activation(s_abs[:, c % 2, :], s_adj[:, c % 2, :], ACT.Abs).then_inc(abs_done, 1)

            def exponent(t, c):
                if c == 0:
                    act.wait_ge(bias_done, t + 1)
                if not is0(t):
                    act.wait_ge(pT_mm, t * C - C + c + 1)
                nc.scalar.activation(prob[:, c * CW:(c + 1) * CW], w[:, c * CW:(c + 1) * CW], ACT.Exp,
                                     bias=exp_bias[:, :], scale=1.0 / SS,
                                     accum_out=sum_part[:, c:c + 1]).then_inc(exp_done, 1)

            def high_half(t, c):
                act.wait_ge(pT_mm, t * C + c + 1)
                if not (is0(t) and c < 2):
                    act.wait_ge(pv_mm, t * C + c - 1)
                nc.scalar.activation(pT[:, c % 2, 0], pT_bank(c).rearrange("p (m n) -> p m n", m=MT),
                                     ACT.Copy).then_inc(pT_hi, 1)

            act.wait_ge(proj_lo, G * 8)
            act.wait_ge(q_stored, G * 16)
            for c in range(C):
                absolute(0, c)

            def attend(t):
                for c in range(4):
                    exponent(t - 1, c)
                absolute(t, 0)
                for c in range(4, 6):
                    exponent(t - 1, c)
                absolute(t, 1)
                for c in range(6, C):
                    exponent(t - 1, c)
                for c in range(C):
                    high_half(t - 1, c)
                    if c + 2 < C:
                        absolute(t, c + 2)

            attend(1)
            with act.Fori(2, T) as t:
                attend(t)
            for c in range(C):
                exponent(T - 1, c)
            for c in range(C):
                high_half(T - 1, c)

            def expert_hi(e):
                act.wait_ge(we_loaded[e % 2], 16 * (e // 2 + 1))
                nc.scalar.activation(we[:, 0, e], we_in[:, e % 2], ACT.Copy, scale=WS).then_inc(we_hi, 1)

            def prep(t, b):
                act.wait_ge(ynT_mm, t + 1)
                if not is0(t):
                    if not (isinstance(t, int) and t == 1):
                        act.wait_ge(y_mm, t * E - E)
                    act.wait_ge(gate_mm, t)
                src = ynT_bank.rearrange("p (k n) -> p k n", k=KC)
                nc.scalar.activation(ynT[:, b, 0], src, ACT.Copy)
                nc.scalar.activation(ynT32, src, ACT.Copy).then_inc(ynT_act, 1)
                act.wait_ge(gate_step, t * 8 + 5)
                nc.scalar.activation(egap[:, :], gap[:, :], ACT.Exp).then_inc(egap_done, 1)
                act.wait_ge(gateT_mm, t + 1)
                nc.scalar.activation(gatesT[:, :], gateT_bank, ACT.Copy).then_inc(gateT_out, 1)

            expert_hi(0)
            expert_hi(1)
            prep(0, 0)
            for e in range(2, E):
                expert_hi(e)
            prep(1, 1)
            with act.Fori(1, T // 2) as i:
                prep(i * 2, 0)
                prep(i * 2 + 1, 1)

        @block.vector
        def _(dve):
            def settle():
                dve.sem_inc(wait_passed, 1)

            nc.vector.memset(ones[:, :], 1.0).then_inc(ones_ready, 1)
            dve.wait_ge(ones_ready, 1)
            dve.wait_ge(b_loaded, 16 * 7)
            for i, col in ((0, bk_col), (1, bv_col)):
                for k in range(KC):
                    last = nc.vector.tensor_scalar(x_wide[i][:, k, :], ones[:, :], col[:, k:k + 1], None, ALU.mult)
            last.then_inc(bias_cols_wide, 1)
            for i in range(2 * KC):
                dve.wait_ge(fold_hi, i + 1)
                f = foldA if i < KC else foldV
                nc.vector.scalar_tensor_tensor(f[:, 1, i % KC, :], ps[:, i, :], WS, f[:, 0, i % KC, :],
                                               ALU.mult, ALU.subtract).then_inc(fold_out, 1)
            dve.wait_ge(fold_mm, 2 * KC + 1)
            nc.vector.tensor_scalar(g_row, ps[:, 0, :], WS, None, ALU.mult).then_inc(fold_out, 1)
            dve.wait_ge(fold_mm, 2 * KC + 2)
            nc.vector.tensor_copy(c_row[:, :], ps[:, 1, :]).then_inc(fold_out, 1)
            dve.wait_ge(fold_mm, 2 * KC + 3)
            nc.vector.tensor_scalar(u_col[:, :], ps[:, 2, 0:KC], WS, None, ALU.mult)
            nc.vector.tensor_scalar(c0[:, :], ps[:, 2, KC:KC + 1], WS, None, ALU.mult).then_inc(fold_out, 1)
            dve.wait_ge(fold_out, 2 * KC + 3)

            def split_values(g):
                dve.wait_ge(val_hi, g + 1)
                nc.vector.tensor_tensor(vT[:, 1], val_in, vT[:, 0], ALU.subtract).then_inc(val_lo, 1)

            def normalize(g):
                dve.wait_ge(x_loaded, g * 16 + 16)
                for s in range(GT):
                    last = nc.vector.bn_stats(stats[:, s, :], x_in[:, s, :])
                last.then_inc(stats_done, 1)
                dve.wait_ge(stats_done, g + 1)
                settle()
                for s in range(GT):
                    last = nc.vector.bn_aggr(moments[:, s, :], stats[:, s, :])
                last.then_inc(moments_done, 1)
                dve.wait_ge(moments_done, g + 1)
                nc.vector.tensor_scalar(var_eps[:, :], moments[:, :, 1], EPS, None, ALU.add).then_inc(var_done, 1)
                dve.wait_ge(rstd_done, g + 1)
                for s in range(GT):
                    nc.vector.tensor_scalar(x_in[:, s, :], x_in[:, s, :], moments[:, s, 0:1], rstd[:, s:s + 1],
                                            ALU.subtract, ALU.mult).then_inc(xn_done, 1)

            def project(g, last=False):
                for s in range(GT):
                    dve.wait_ge(xnT_hi, g * GT + s + 1)
                    nc.vector.tensor_tensor(xnT[:, 1, :, s * P:(s + 1) * P],
                                            tr_bank(s).rearrange("p (k n) -> p k n", k=KC),
                                            xnT[:, 0, :, s * P:(s + 1) * P], ALU.subtract).then_inc(xnT_lo, 1)
                    dve.wait_ge(proj_hi, g * 8 + s + 1)
                    nc.vector.tensor_tensor(v[:, 1, g * GT + s, :], mm_bank(s), v[:, 0, g * GT + s, :],
                                            ALU.subtract).then_inc(proj_lo, 1)
                    dve.wait_ge(xn_done, g * GT + s + 1)
                    if not (is0(g) and s == 0):
                        dve.wait_ge(r_done, g * GT + s)
                    settle()
                    nc.vector.tensor_tensor_reduce(out=r_junk, in0=x_in[:, s, :], in1=g_row, scale=1.0,
                                                   scalar=c0[:, :], op0=ALU.mult, op1=ALU.add,
                                                   accum_out=r_tmp[:, s:s + 1]).then_inc(r_done, 1)
                dve.wait_ge(key_hi, g + 1)
                nc.vector.tensor_tensor(kT[:, 1, :, bass.ds(g * GW, GW)], key_in, kT[:, 0, :, bass.ds(g * GW, GW)],
                                        ALU.subtract).then_inc(key_lo, 1)
                dve.wait_ge(r_done, g * GT + GT)
                nc.vector.tensor_copy(r_all[:, bass.ds(g * GT, GT)], r_tmp[:, :]).then_inc(r_kept, 1)
                for j in range(KC):
                    if j == 1 and not last:
                        split_values(g + 1)
                    dve.wait_ge(proj_hi, g * 8 + 4 + j + 1)
                    nc.vector.scalar_tensor_tensor(q_out[:, :, 1, j, :],
                                                   mm_bank(j).rearrange("p (t n) -> p t n", t=GT),
                                                   u_col[:, j:j + 1], q_out[:, :, 0, j, :],
                                                   ALU.add, ALU.subtract).then_inc(proj_lo, 1)
                if not last:
                    normalize(g + 1)

            split_values(0)
            normalize(0)
            project(0)
            with dve.Fori(1, G - 1) as g:
                project(g)
            project(G - 1, last=True)
            dve.wait_ge(r_kept, G)
            dve.wait_ge(q_stored, G * 16)

            def row_consts(t):
                nc.vector.tensor_copy(r_cur[:, :], r_all[:, bass.ds(t, 1)]).then_inc(rcur_done, 1)
                dve.wait_ge(rcur_done, t + 1)

            def times_adj(t, c):
                dve.wait_ge(s_mm, t * C + c + 1)
                dve.wait_ge(adj_loaded[c], t * 16 + 16)
                nc.vector.scalar_tensor_tensor(s_adj[:, c % 2, :], s_bank(c), r_cur[:, :], adj_in[:, c, :],
                                               ALU.add, ALU.mult).then_inc(s_read, 1)

            def mask(t, c):
                dve.wait_ge(abs_done, t * C + c + 1)
                nc.vector.tensor_scalar(s_abs[:, c % 2, :], s_abs[:, c % 2, :], THRESHOLD * SS, NEG * SS,
                                        ALU.is_lt, ALU.mult).then_inc(mask_done, 1)
                dve.wait_ge(mask_done, t * C + c + 1)
                if not is0(t):
                    dve.wait_ge(exp_done, t * C - C + c + 1)
                settle()
                nc.vector.tensor_tensor_reduce(out=w[:, c * CW:(c + 1) * CW], in0=s_adj[:, c % 2, :],
                                               in1=s_abs[:, c % 2, :], scale=1.0, scalar=-3.0e38,
                                               op0=ALU.add, op1=ALU.max,
                                               accum_out=max_part[:, c:c + 1]).then_inc(w_done, 1)

            def softmax_bias(t):
                dve.wait_ge(w_done, t * C + C)
                nc.vector.reduce_max(row_max[:, :], max_part[:, :], AX_X).then_inc(max_done, 1)
                dve.wait_ge(max_done, t + 1)
                nc.vector.tensor_scalar(exp_bias[:, :], row_max[:, :], -1.0 / SS, None, ALU.mult).then_inc(bias_done, 1)

            def low_half(t, c):
                dve.wait_ge(pT_hi, t * C + c + 1)
                nc.vector.tensor_tensor(pT[:, c % 2, 1], pT_bank(c).rearrange("p (m n) -> p m n", m=MT),
                                        pT[:, c % 2, 0], ALU.subtract).then_inc(pT_lo, 1)

            def inverse_sum(t):
                dve.wait_ge(exp_done, t * C + C)
                nc.vector.reduce_sum(row_sum[:, :], sum_part[:, :], AX_X).then_inc(sum_done, 1)
                dve.wait_ge(sum_done, t + 1)
                nc.vector.tensor_scalar(row_sum_ws[:, :], row_sum[:, :], WS, None, ALU.mult).then_inc(sum_ws_done, 1)
                dve.wait_ge(sum_ws_done, t + 1)
                nc.vector.reciprocal(inv_sum[:, :], row_sum_ws[:, :]).then_inc(inv_done, 1)
                dve.wait_ge(xres_loaded, t * 16 + 16)
                nc.vector.tensor_tensor(x_res, x_res, c_row[:, :], ALU.add).then_inc(xc_done, 1)

            def residual(t):
                dve.wait_ge(xc_done, t + 1)
                dve.wait_ge(inv_done, t + 1)
                dve.wait_ge(pv_mm, t * C + C)
                if not is0(t):
                    dve.wait_ge(x1_stored, t * 16)
                nc.vector.scalar_tensor_tensor(x1_out, o_bank, inv_sum[:, :], x_res, ALU.mult,
                                               ALU.add).then_inc(x1_done, 1)

            row_consts(0)
            for c in range(C):
                times_adj(0, c)
                mask(0, c)
            softmax_bias(0)
            def attend(t):
                row_consts(t)
                times_adj(t, 0)
                times_adj(t, 1)
                for c in range(C):
                    if c == 0:
                        mask(t, 0)
                    elif c + 1 < C:
                        mask(t, c + 1)
                    if c == 2:
                        inverse_sum(t - 1)
                    if c == C - 2:
                        softmax_bias(t)
                    low_half(t - 1, c)
                    if c == 0:
                        mask(t, 1)
                    if c + 2 < C:
                        times_adj(t, c + 2)
                residual(t - 1)

            attend(1)
            with dve.Fori(2, T) as t:
                attend(t)
            inverse_sum(T - 1)
            for c in range(C):
                low_half(T - 1, c)
            residual(T - 1)

            def expert_lo(e):
                dve.wait_ge(we_hi, e + 1)
                nc.vector.scalar_tensor_tensor(we[:, 1, e].rearrange("p k o -> p (k o)"),
                                               we_in[:, e % 2].rearrange("p k o -> p (k o)"), WS,
                                               we[:, 0, e].rearrange("p k o -> p (k o)"),
                                               ALU.mult, ALU.subtract).then_inc(we_lo, 1)

            def prep_norm(t, b, n):
                dve.wait_ge(y_loaded[b], n * 16 + 16)
                nc.vector.bn_stats(stats[:, 0, :], y_in[:, b]).then_inc(ystats_done, 1)
                dve.wait_ge(ystats_done, t + 1)
                settle()
                nc.vector.bn_aggr(moments[:, 0, :], stats[:, 0, :]).then_inc(ymom_done, 1)
                dve.wait_ge(ymom_done, t + 1)
                nc.vector.tensor_scalar(var_eps[:, 0:1], moments[:, 0, 1:2], EPS, None, ALU.add).then_inc(yvar_done, 1)
                dve.wait_ge(yrstd_done, t + 1)
                if not is0(t):
                    dve.wait_ge(ynT_mm, t)
                nc.vector.tensor_scalar(yn, y_in[:, b], moments[:, 0, 0:1], rstd[:, 0:1],
                                        ALU.subtract, ALU.mult).then_inc(yn_done, 1)

            def prep_split(t, b):
                dve.wait_ge(ynT_act, t + 1)
                nc.vector.tensor_tensor(ynT[:, b, 1], ynT_bank.rearrange("p (k n) -> p k n", k=KC), ynT[:, b, 0],
                                        ALU.subtract).then_inc(ynT_lo, 1)

            def prep_gates(t, b):
                n = [0]

                def step(ins):
                    n[0] += 1
                    ins.then_inc(gate_step, 1)
                    dve.wait_ge(gate_step, t * 8 + n[0])

                dve.wait_ge(gate_mm, t + 1)
                step(nc.vector.tensor_copy(logits[:, :], gate_bank))
                settle()
                step(nc.vector.max(top8[:, :], logits[:, :]))
                settle()
                step(nc.vector.max_index(top_idx[:, :], top8[:, :], logits[:, :]))
                step(nc.vector.tensor_copy(top_idx_f[:, :], top_idx[:, :]))
                step(nc.vector.tensor_tensor(gap[:, :], top8[:, 1:2], top8[:, 0:1], ALU.subtract))
                dve.wait_ge(egap_done, t + 1)
                step(nc.vector.tensor_scalar(den[:, :], egap[:, :], 1.0, None, ALU.add))
                step(nc.vector.reciprocal(gate[:, 0:1], den[:, :]))
                step(nc.vector.tensor_tensor(gate[:, 1:2], gate[:, 0:1], egap[:, :], ALU.mult))
                nc.vector.tensor_scalar(gate_1[:, :], iota_e[:, :], top_idx_f[:, 0:1], gate[:, 0:1],
                                        ALU.is_equal, ALU.mult)
                nc.vector.tensor_scalar(gate_2[:, :], iota_e[:, :], top_idx_f[:, 1:2], gate[:, 1:2],
                                        ALU.is_equal, ALU.mult).then_inc(gates_done, 1)
                dve.wait_ge(gates_done, t * 3 + 1)
                nc.vector.tensor_tensor(gates[:, :], gate_1[:, :], gate_2[:, :], ALU.add).then_inc(gates_done, 1)
                dve.wait_ge(gates_done, t * 3 + 2)
                nc.vector.tensor_scalar(gates_ws[:, b], gates[:, :], 1.0 / WS, None, ALU.mult).then_inc(gates_done, 1)

            def start_acc(t, b, n):
                dve.wait_ge(bias_mm, t + 1)
                dve.wait_ge(gates_done, t * 3 + 3)
                if not (isinstance(n, int) and n == 0):
                    dve.wait_ge(out_stored[b], n * 16)
                nc.vector.tensor_tensor(acc[:, b], bias_bank, y_in[:, b], ALU.add).then_inc(acc_start, 1)
                dve.wait_ge(acc_start, t + 1)

            def add_expert(t, b, e):
                dve.wait_ge(y_mm, t * E + e + 1)
                if not (is0(t) and e == 0):
                    dve.wait_ge(y_added, t * E + e)
                nc.vector.scalar_tensor_tensor(acc[:, b], y_bank(e), gates_ws[:, b, e:e + 1], acc[:, b],
                                               ALU.mult, ALU.add).then_inc(y_added, 1)

            def experts(t, b, n, last):
                start_acc(t, b, n)
                for e in range(E):
                    if is0(t) and e + 2 < E:
                        expert_lo(e + 2)
                    add_expert(t, b, e)
                    if not last:
                        nb = n + b
                        if e == 1:
                            prep_norm(t + 1, 1 - b, nb)
                        if e == 3:
                            prep_split(t + 1, 1 - b)
                        if e == 4:
                            prep_gates(t + 1, 1 - b)

            expert_lo(0)
            expert_lo(1)
            prep_norm(0, 0, 0)
            prep_split(0, 0)
            prep_gates(0, 0)
            experts(0, 0, 0, False)
            experts(1, 1, 0, False)
            with dve.Fori(1, T // 2 - 1) as i:
                experts(i * 2, 0, i, False)
                experts(i * 2 + 1, 1, i, False)
            experts(T - 2, 0, T // 2 - 1, False)
            experts(T - 1, 1, T // 2 - 1, True)

        @block.tensor
        def _(pe):
            def product(bank, pairs):
                n = len(pairs)
                for k, (st, mv) in enumerate(pairs):
                    nc.tensor.matmul(bank, st[0], mv[0], start=(k == 0), stop=False)
                    nc.tensor.matmul(bank, st[0], mv[1], start=False, stop=False)
                    last = nc.tensor.matmul(bank, st[1], mv[0], start=False, stop=(k == n - 1))
                return last

            def exact(bank, pairs):
                n = len(pairs)
                for k, (st, mv) in enumerate(pairs):
                    last = nc.tensor.matmul(bank, st, mv, start=(k == 0), stop=(k == n - 1))
                return last

            pe.wait_ge(w_loaded, 64)
            for i in range(KC):
                exact(ps[:, i, :], [(wq_raw[:, o, i * P:(i + 1) * P], wk_raw[:, o, :])
                                    for o in range(KC)]).then_inc(fold_mm, 1)
            for i in range(KC):
                exact(ps[:, KC + i, :], [(wv_raw[:, o, i * P:(i + 1) * P], wmT_raw[:, o, :])
                                         for o in range(KC)]).then_inc(fold_mm, 1)
            pe.wait_ge(bias_cols_wide, 1)
            pe.wait_ge(fold_out, 1)
            exact(ps[:, 0, :], [(x_wide[0][:, o, :], wq_raw[:, o, :]) for o in range(KC)]).then_inc(fold_mm, 1)
            pe.wait_ge(fold_out, 2)
            exact(ps[:, 1, :], [(x_wide[1][:, o, :], wmT_raw[:, o, :]) for o in range(KC)]
                  + [(ones[0:1, :], bm_row[:, :])]).then_inc(fold_mm, 1)
            pe.wait_ge(fold_out, 3)
            for j in range(KC):
                exact(ps[:, 2, j:j + 1], [(wk_raw[:, o, j * P:(j + 1) * P], bq_col[:, o:o + 1]) for o in range(KC)])
            exact(ps[:, 2, KC:KC + 1], [(x_wide[0][:, o, :], bq_col[:, o:o + 1])
                                        for o in range(KC)]).then_inc(fold_mm, 1)

            pe.wait_ge(fold_out, 2 * KC + 3)
            pe.wait_ge(consts_ready, 2)

            def project(g):
                def turn(s):
                    pe.wait_ge(xn_done, g * GT + s + 1)
                    if not is0(g):
                        pe.wait_ge(xnT_lo, g * GT + s - 3)
                    for k in range(KC):
                        last = nc.tensor.transpose(tr_bank(s)[:, k * P:(k + 1) * P],
                                                   x_in[:, s, k * P:(k + 1) * P], ident[:, :])
                    last.then_inc(xnT_mm, 1)

                for s in range(GT):
                    if s == 0:
                        pe.wait_ge(val_lo, g + 1)
                    if not is0(g):
                        pe.wait_ge(proj_lo, g * 8 - 4 + s + 1)
                    product(mm_bank(s), [((vT[:, 0, k, s * P:(s + 1) * P], vT[:, 1, k, s * P:(s + 1) * P]),
                                          (foldV[:, 0, k, :], foldV[:, 1, k, :])) for k in range(KC)]
                            ).then_inc(proj_mm, 1)
                    turn(s)
                for j in range(KC):
                    if j == 0:
                        pe.wait_ge(xnT_lo, g * GT + GT)
                    pe.wait_ge(proj_lo, g * 8 + j + 1)
                    product(mm_bank(j), [((foldA[:, 0, k, j * P:(j + 1) * P], foldA[:, 1, k, j * P:(j + 1) * P]),
                                          (xnT[:, 0, k, :], xnT[:, 1, k, :])) for k in range(KC)]
                            ).then_inc(proj_mm, 1)

            project(0)
            with pe.Fori(1, G) as g:
                project(g)
            pe.wait_ge(key_lo, G)
            pe.wait_ge(proj_lo, G * 8)
            pe.wait_ge(xnT_lo, G * GT)

            def scores(t, c):
                if c == 0:
                    pe.wait_ge(q_loaded, t * 16 + 16)
                if not (is0(t) and c < 2):
                    pe.wait_ge(s_read, t * C + c - 1)
                product(s_bank(c), [((q_in[:, 0, k, :], q_in[:, 1, k, :]),
                                     (kT[:, 0, k, c * CW:(c + 1) * CW], kT[:, 1, k, c * CW:(c + 1) * CW]))
                                    for k in range(KC)]).then_inc(s_mm, 1)

            def turn_probs(t, c):
                pe.wait_ge(exp_done, t * C + c + 1)
                if not (is0(t) and c < 2):
                    pe.wait_ge(pT_lo, t * C + c - 1)
                for m in range(MT):
                    at = c * CW + m * P
                    last = nc.tensor.transpose(pT_bank(c)[:, m * P:(m + 1) * P], prob[:, at:at + P], ident[:, :])
                last.then_inc(pT_mm, 1)

            def times_values(t, c):
                pe.wait_ge(pT_lo, t * C + c + 1)
                if c == 0 and not is0(t):
                    pe.wait_ge(x1_done, t)
                for m in range(MT):
                    st = (pT[:, c % 2, 0, m, :], pT[:, c % 2, 1, m, :])
                    mv = (v[:, 0, c * MT + m, :], v[:, 1, c * MT + m, :])
                    first, final = c == 0 and m == 0, c == C - 1 and m == MT - 1
                    nc.tensor.matmul(o_bank, st[0], mv[0], start=first, stop=False)
                    nc.tensor.matmul(o_bank, st[0], mv[1], start=False, stop=False)
                    last = nc.tensor.matmul(o_bank, st[1], mv[0], start=False, stop=final)
                last.then_inc(pv_mm, 1)

            def attend(t):
                scores(t, 0)
                scores(t, 1)
                for c in range(C):
                    turn_probs(t - 1, c)
                    if c + 2 < C:
                        scores(t, c + 2)
                    if c >= 1:
                        times_values(t - 1, c - 1)
                times_values(t - 1, C - 1)

            for c in range(C):
                scores(0, c)
            attend(1)
            with pe.Fori(2, T) as t:
                attend(t)
            for c in range(C):
                turn_probs(T - 1, c)
                if c >= 1:
                    times_values(T - 1, c - 1)
            times_values(T - 1, C - 1)

            def prep_turn(t):
                pe.wait_ge(yn_done, t + 1)
                if not is0(t):
                    pe.wait_ge(ynT_lo, t)
                for k in range(KC):
                    last = nc.tensor.transpose(ynT_bank[:, k * P:(k + 1) * P], yn[:, k * P:(k + 1) * P], ident[:, :])
                last.then_inc(ynT_mm, 1)

            def prep_gate(t):
                pe.wait_ge(ynT_act, t + 1)
                if not is0(t):
                    pe.wait_ge(gateT_out, t)
                exact(gate_bank, [(ynT32[:, k, :], wg[:, k, :]) for k in range(KC)]
                      + [(ones[0:1, :], bg_row[:, :])]).then_inc(gate_mm, 1)

            def prep_gateT(t):
                pe.wait_ge(gates_done, t * 3 + 3)
                nc.tensor.transpose(gateT_bank, gates[:, :], ident[:, :]).then_inc(gateT_mm, 1)

            def prep_bias(t):
                pe.wait_ge(gateT_out, t + 1)
                if not is0(t):
                    pe.wait_ge(acc_start, t)
                nc.tensor.matmul(bias_bank, gatesT[:, :], be_in[:, :], start=True, stop=True).then_inc(bias_mm, 1)

            def experts(t, b, last):
                for e in range(E):
                    if is0(t):
                        pe.wait_ge(we_lo, e + 1)
                    if e == 0:
                        pe.wait_ge(ynT_lo, t + 1)
                    if not (is0(t) and e < 4):
                        pe.wait_ge(y_added, t * E + e - 3)
                    product(y_bank(e), [((ynT[:, b, 0, k, :], ynT[:, b, 1, k, :]),
                                         (we[:, 0, e, k, :], we[:, 1, e, k, :])) for k in range(KC)]
                            ).then_inc(y_mm, 1)
                    if not last:
                        if e == 2:
                            prep_turn(t + 1)
                        if e == 4:
                            prep_gate(t + 1)
                        if e == 6:
                            prep_gateT(t + 1)
                        if e == 7:
                            prep_bias(t + 1)

            prep_turn(0)
            prep_gate(0)
            prep_gateT(0)
            prep_bias(0)
            experts(0, 0, False)
            experts(1, 1, False)
            with pe.Fori(1, T // 2 - 1) as i:
                experts(i * 2, 0, False)
                experts(i * 2 + 1, 1, False)
            experts(T - 2, 0, False)
            experts(T - 1, 1, True)


def kernel(x, adj, L0_gnn_key, L0_gnn_value, L0_gnn_Wq, L0_gnn_bq, L0_gnn_Wk, L0_gnn_bk, L0_gnn_Wv, L0_gnn_bv,
           L0_gnn_Wm, L0_gnn_bm, L0_ffn_Wg, L0_ffn_bg, L0_ffn_We, L0_ffn_be):
    import numpy as np
    import concourse.bacc as bacc
    from concourse.bass_utils import run_bass_kernel_spmd

    nc = bacc.Bacc("TRN2", target_bir_lowering=False, num_devices=1)
    laid_out = {
        "x": x, "adj": adj,
        "keyT": np.asarray(L0_gnn_key).T, "valueT": np.asarray(L0_gnn_value).T,
        "Wq": L0_gnn_Wq, "bq": L0_gnn_bq, "Wk": L0_gnn_Wk, "bk": L0_gnn_bk, "Wv": L0_gnn_Wv, "bv": L0_gnn_bv,
        "WmT": np.asarray(L0_gnn_Wm).T, "bm": L0_gnn_bm,
        "Wg": L0_ffn_Wg, "bg": L0_ffn_bg,
        "WeT": np.asarray(L0_ffn_We).transpose(0, 2, 1), "be": L0_ffn_be,
    }
    arrays, args = {}, []
    for name, a in laid_out.items():
        a = np.ascontiguousarray(a)
        arrays[f"in_{name}"] = a
        args.append(nc.dram_tensor(f"in_{name}", a.shape, mybir.dt.from_np(a.dtype), kind="ExternalInput").ap())
    result = nc.dram_tensor("out_0", tuple(x.shape), mybir.dt.float32, kind="ExternalOutput").ap()
    graph_attention_moe_kernel(nc, *args, result)
    r = run_bass_kernel_spmd(nc, [arrays], core_ids=[0])
    return r.results[0]["out_0"]
```

```python
from contextlib import ExitStack

import concourse.bass as bass
from concourse import mybir

F32 = mybir.dt.float32
F16 = mybir.dt.float16
U32 = mybir.dt.uint32
ALU = mybir.AluOpType
ACT = mybir.ActivationFunctionType
AX_X = mybir.AxisListType.X

P = 128
NEG = -1e9
THRESHOLD = 1e-5
EPS = 1e-5
WS = 16.0


def graph_attention_moe_kernel(nc, x, adj, keyT, valueT, Wq, bq, Wk, bk, Wv, bv, WmT, bm, Wg, bg, WeT, be, outs):
    N, D = x.shape
    E = WeT.shape[0]
    KC = D // P
    T = N // P
    GT = D // P
    G = T // GT
    GW = GT * P
    CW = 512
    C = N // CW
    MT = CW // P
    HALVES = len(outs)
    TH = T // HALVES
    NH = N // HALVES
    REGION = TH + 1
    DUMMY = E * REGION
    BLOCKS = (2 * NH + E * (P - 1)) // P
    LEAD = 11
    ROW = D + 2
    RING = 4
    GATE_STEPS, PICK_STEPS, SLOT_STEPS = 8, 2, 5
    TURNS_AFTER = ((), (0, 1), (2, 3), ())
    TABLE_STEPS = 11
    assert (BLOCKS - LEAD) % 2 == 0 and (T % HALVES) == 0
    SPLIT_EARLY = C
    PADS_AFTER = {8: range(0, 4), 9: range(4, 8)}
    assert 2 * E - SPLIT_EARLY <= LEAD
    SS = WS * float(N) ** 0.5
    assert D == 512 and GW == 512 and SS == 1024.0

    ctx = ExitStack()
    with ctx:
        def sb(name, shape, dt):
            return ctx.enter_context(nc.sbuf_tensor(name, shape, dt))

        def sem(name):
            return ctx.enter_context(nc.semaphore(name))

        key_region = sb("key_region", [P, 2 * KC * N], F16)
        val_region = sb("val_region", [P, 2 * T * D], F16)
        work = sb("work", [P, 17924], F32)

        kT = key_region[:, :].rearrange("p (h k n) -> p h k n", h=2, k=KC)
        v = val_region[:, :].rearrange("p (h t d) -> p h t d", h=2, t=T)
        we = key_region[:, :].rearrange("p (h e k o) -> p h e k o", h=2, e=E, k=KC)
        raw = val_region[:, 0:8 * KC * D].bitcast(F32).rearrange("p (w k d) -> p w k d", w=4, k=KC)
        wq_raw, wk_raw, wv_raw, wmT_raw = (raw[:, i] for i in range(4))

        taken = [0]

        def carve(words):
            at = taken[0]
            taken[0] += words
            assert taken[0] <= 17924, taken
            return work[:, at:at + words]

        foldA = carve(KC * D).bitcast(F16).rearrange("p (h k d) -> p h k d", h=2, k=KC)
        foldV = carve(KC * D).bitcast(F16).rearrange("p (h k d) -> p h k d", h=2, k=KC)
        key_in = carve(KC * GW).rearrange("p (k n) -> p k n", k=KC)
        val_in = carve(KC * GW).rearrange("p (k n) -> p k n", k=KC)
        x_in = carve(GT * D).rearrange("p (t d) -> p t d", t=GT)
        vT = carve(KC * GW).bitcast(F16).rearrange("p (h k n) -> p h k n", h=2, k=KC)
        xnT = carve(KC * GW).bitcast(F16).rearrange("p (h k n) -> p h k n", h=2, k=KC)
        r_junk = carve(D)
        q_out = carve(KC * GW).bitcast(F16).rearrange("p (t h k n) -> p t h k n", t=GT, h=2, k=KC)
        g_row = carve(D)
        bm_row = r_junk[0:1, :]
        x_wide = [q_out.rearrange("p t h k n -> p (t h k n)").bitcast(F32)[:, i * D:(i + 1) * D]
                  .rearrange("p (k n) -> p k n", k=KC) for i in range(2)]
        taken[0] = 0
        w = carve(N)
        prob = carve(N)
        adj_in = carve(N).rearrange("p (c n) -> p c n", c=C)
        s_adj = carve(2 * CW).rearrange("p (b n) -> p b n", b=2)
        s_abs = carve(2 * CW).rearrange("p (b n) -> p b n", b=2)
        q_in = carve(KC * P).bitcast(F16).rearrange("p (h k n) -> p h k n", h=2, k=KC)
        pT = carve(2 * MT * P).bitcast(F16).rearrange("p (b h m n) -> p b h m n", b=2, h=2, m=MT)
        x_res = carve(D)
        x1_out = carve(D)
        row_buf = carve(ROW)
        ynT_words = carve(KC * P)
        ynT32 = ynT_words.rearrange("p (k n) -> p k n", k=KC)
        q_in1 = ynT_words.bitcast(F16).rearrange("p (h k n) -> p h k n", h=2, k=KC)
        taken[0] = 0
        be_all = carve(E * D).rearrange("p (e d) -> p e d", e=E)
        y_out = carve(RING * D).rearrange("p (b d) -> p b d", b=RING)
        y_tmp = carve(2 * D).rearrange("p (b d) -> p b d", b=2)
        carve(N - RING * D - 2 * D)
        we_in = carve(2 * KC * D).rearrange("p (b k o) -> p b k o", b=2, k=KC)
        tok_in = carve(2 * ROW).rearrange("p (b d) -> p b d", b=2)
        tokT = carve(2 * KC * P).bitcast(F16).rearrange("p (b h k n) -> p b h k n", b=2, h=2, k=KC)
        assert taken[0] <= 3 * N + 4 * CW + KC * P

        ident = sb("ident", [P, P], F32)
        ones = sb("ones", [P, P], F32)
        neg_half = sb("neg_half", [P, GT], F32)
        c_row = sb("c_row", [P, D], F32)
        bq_col = sb("bq_col", [P, KC], F32)
        bk_col = sb("bk_col", [P, KC], F32)
        bv_col = sb("bv_col", [P, KC], F32)
        bg_row = sb("bg_row", [1, E], F32)
        wg = sb("wg", [P, KC, E], F32)
        u_col = sb("u_col", [P, KC], F32)
        c0 = sb("c0", [P, 1], F32)
        r_tmp = sb("r_tmp", [P, GT], F32)
        r_all = sb("r_all", [P, T], F32)
        r_cur = sb("r_cur", [P, 1], F32)
        stats = sb("stats", [P, GT, 6], F32)
        moments = sb("moments", [P, GT, 2], F32)
        var_eps = sb("var_eps", [P, GT], F32)
        rstd = sb("rstd", [P, GT], F32)
        max_part = sb("max_part", [P, C], F32)
        row_max = sb("row_max", [P, 1], F32)
        exp_bias = sb("exp_bias", [P, 1], F32)
        sum_part = sb("sum_part", [P, C], F32)
        row_sum = sb("row_sum", [P, 1], F32)
        row_sum_ws = sb("row_sum_ws", [P, 1], F32)
        inv_sum = sb("inv_sum", [P, 1], F32)
        iota_e = sb("iota_e", [P, E], F32)
        logits = sb("logits", [P, E], F32)
        top8 = sb("top8", [P, 8], F32)
        top_idx = sb("top_idx", [P, 8], U32)
        top_idx_f = sb("top_idx_f", [P, 8], F32)
        gap = sb("gap", [P, 1], F32)
        egap = sb("egap", [P, 1], F32)
        den = sb("den", [P, 1], F32)
        gate = sb("gate", [P, 2], F32)
        pick = sb("pick", [P, 2, E], F32)
        picked = sb("picked", [P, E], F32)
        tri = sb("tri", [P, P], F32)
        row_ids = sb("row_ids", [P, TH], F32)
        pad_row = sb("pad_row", [P, ROW], F32)
        region_start = sb("region_start", [P, E], F32)
        next_slot = sb("next_slot", [P, E], F32)
        slot_of = sb("slot_of", [P, E], F32)
        slot_junk = sb("slot_junk", [P, E], F32)
        slots_f = sb("slots_f", [P, 2], F32)
        slots_u = sb("slots_u", [P, 2], U32)
        blocks_u = sb("blocks_u", [1, E], U32)
        blocks_f = [sb(f"blocks_f{i}", [1, E + E // 2], F32) for i in range(2)]
        region_gap = sb("region_gap", [1, E], F32)
        iota_k = sb("iota_k", [1, BLOCKS], F32)
        behind = sb("behind", [1, BLOCKS, E], F32)
        tab_f = sb("tab_f", [1, 2, BLOCKS], F32)
        pad_at = sb("pad_at", [1, HALVES, E], U32)
        tab_row = sb("tab_row", [1, HALVES, BLOCKS], U32)
        tab_expert = sb("tab_expert", [1, HALVES, BLOCKS], U32)
        tok_ids = sb("tok_ids", [P, RING], U32)
        tok_gates = sb("tok_gates", [P, RING], F32)

        ps = ctx.enter_context(nc.psum_tensor("ps", [P, 8, 512], F32))
        tr_bank = lambda i: ps[:, i % 4, :]
        mm_bank = lambda i: ps[:, 4 + i % 4, :]
        s_bank = lambda c: ps[:, c % 2, :]
        pT_bank = lambda c: ps[:, 2 + c % 2, :]
        o_bank = ps[:, 4, :]
        ynT_bank = ps[:, 5, :]
        gate_bank = ps[:, 6, 0:E]
        rank_bank = ps[:, 6, 16:16 + E]
        count_bank = ps[:, 6, 32:32 + E]
        tokT_bank = lambda b: ps[:, b, :]
        y_bank = lambda b: ps[:, 2 + b, :]

        q_dram = nc.dram_tensor("q_scratch", (T, P, 2 * KC * P), F16, kind="Internal").ap()
        slots = [nc.dram_tensor(f"slots{h}", ((DUMMY + 1) * P, ROW), F32, kind="Internal").ap() for h in range(HALVES)]
        x_tiles = x.rearrange("(t p) d -> t p d", p=P)
        x_groups = x.rearrange("(t p) d -> p t d", p=P)
        keyT_v = keyT.rearrange("(k p) n -> p k n", p=P)
        valueT_v = valueT.rearrange("(k p) n -> p k n", p=P)
        adj_tiles = adj.rearrange("(t p) n -> t p n", p=P)
        out_tiles = [o.rearrange("(t p) d -> t p d", p=P) for o in outs]
        weT_v = WeT.rearrange("e (k p) o -> e p k o", p=P)

        wqk_loaded = [sem(f"wqk_loaded{o}") for o in range(KC)]
        wvm_loaded = sem("wvm_loaded")
        b_loaded = sem("b_loaded")
        consts_ready = sem("consts_ready")
        ident_step = sem("ident_step")
        ones_ready = sem("ones_ready")
        wait_passed = sem("wait_passed")
        wait_passed_pool = sem("wait_passed_pool")
        bias_cols_wide = sem("bias_cols_wide")
        fold_mm = sem("fold_mm")
        fold_hi = sem("fold_hi")
        fold_out = sem("fold_out")
        key_loaded = sem("key_loaded")
        key_hi = sem("key_hi")
        key_lo = sem("key_lo")
        val_loaded = sem("val_loaded")
        val_hi = sem("val_hi")
        val_lo = sem("val_lo")
        x_loaded = sem("x_loaded")
        stats_done = sem("stats_done")
        moments_done = sem("moments_done")
        var_done = sem("var_done")
        rstd_done = sem("rstd_done")
        xn_done = sem("xn_done")
        r_done = sem("r_done")
        r_kept = sem("r_kept")
        xnT_mm = sem("xnT_mm")
        xnT_hi = sem("xnT_hi")
        xnT_lo = sem("xnT_lo")
        proj_mm = sem("proj_mm")
        proj_hi = sem("proj_hi")
        proj_lo = sem("proj_lo")
        q_stored = sem("q_stored")
        q_loaded = sem("q_loaded")
        q1_loaded = sem("q1_loaded")
        adj_loaded = [sem(f"adj_loaded{c}") for c in range(C)]
        xres_loaded = sem("xres_loaded")
        rcur_done = sem("rcur_done")
        s_mm = sem("s_mm")
        s_read = sem("s_read")
        abs_done = sem("abs_done")
        mask_done = sem("mask_done")
        w_done = sem("w_done")
        max_done = sem("max_done")
        bias_done = sem("bias_done")
        exp_done = sem("exp_done")
        pT_mm = sem("pT_mm")
        pT_hi = sem("pT_hi")
        pT_lo = sem("pT_lo")
        pv_mm = sem("pv_mm")
        sum_done = sem("sum_done")
        sum_ws_done = sem("sum_ws_done")
        inv_done = sem("inv_done")
        xc_done = sem("xc_done")
        x1_done = sem("x1_done")
        x1_stored = sem("x1_stored")
        we_loaded = [sem(f"we_loaded{b}") for b in range(2)]
        we_hi = sem("we_hi")
        we_lo = sem("we_lo")
        be_loaded = sem("be_loaded")
        pads_ready = sem("pads_ready")
        out_pads = sem("out_pads")
        ystats_done = sem("ystats_done")
        ymom_done = sem("ymom_done")
        yvar_done = sem("yvar_done")
        yrstd_done = sem("yrstd_done")
        yn_done = sem("yn_done")
        ynT_mm = sem("ynT_mm")
        ynT_act = sem("ynT_act")
        gate_mm = sem("gate_mm")
        gate_step = sem("gate_step")
        egap_done = sem("egap_done")
        pick_step = sem("pick_step")
        rank_mm = sem("rank_mm")
        slot_step = sem("slot_step")
        gate_put = sem("gate_put")
        slotted = sem("slotted")
        tables_step = sem("tables_step")
        slots_reset = sem("slots_reset")
        tables_done = sem("tables_done")
        padded = [sem(f"padded{h}") for h in range(HALVES)]
        tok_loaded = [sem(f"tok_loaded{b}") for b in range(2)]
        tok_meta = sem("tok_meta")
        tokT_mm = sem("tokT_mm")
        tokT_hi = sem("tokT_hi")
        tokT_lo = sem("tokT_lo")
        y_mm = sem("y_mm")
        y_biased = sem("y_biased")
        y_scaled = sem("y_scaled")
        y_added = [sem(f"y_added{b}") for b in range(RING)]

        halves_of_k = (slice(0, KC // 2), slice(KC // 2, KC))
        is0 = lambda g: isinstance(g, int) and g == 0
        isl = lambda g, n: isinstance(g, int) and g == n - 1

        class Step:

            def __init__(self, base, j, h, k, alone):
                self.base, self.j, self.h, self.k, self.alone = base, j, h, k, alone
                self.b2, self.b4 = base % 2, base % RING

            def count(self, back=0):
                return self.j * RING + (self.base - back + 1)

            def uses(self, n, back=0):
                return self.j * (RING // n) + ((self.base - back) // n + 1)

            def has(self, back):
                return self.base >= back

        def lead_steps():
            return [Step(s, 0, 0, s, True) for s in range(LEAD)]

        def turn_steps(j):
            return [Step(LEAD + i, j, i % 2, j * 2 + (LEAD if i % 2 == 0 else 0) + i // 2, False)
                    for i in range(RING)]

        TURNS = 2 * (BLOCKS - LEAD) // RING

        def tail_steps():
            first = LEAD + TURNS * RING
            return [Step(first + i, 0, 1, BLOCKS - LEAD + i, True) for i in range(LEAD)]

        block = ctx.enter_context(nc.Block())

        @block.sync
        def _(sp):
            for o in range(KC):
                for dst, src in ((wq_raw, Wq), (wk_raw, Wk)):
                    sp.dma_start(dst[:, o, :], src[o * P:(o + 1) * P, :]).then_inc(wqk_loaded[o], 16)
            with nc.allow_non_contiguous_dma(reason="small bias columns"):
                for col, src in ((bq_col, bq), (bk_col, bk), (bv_col, bv)):
                    sp.dma_start(col[:, :], src.rearrange("(k p) -> p k", p=P)).then_inc(b_loaded, 16)
                sp.dma_start(wg[:, :, :], Wg.rearrange("(k p) e -> p k e", p=P)).then_inc(b_loaded, 16)
            sp.dma_start(bm_row, bm.rearrange("(a d) -> a d", a=1)).then_inc(b_loaded, 16)
            sp.dma_start(bg_row[:, :], bg.rearrange("(a d) -> a d", a=1)).then_inc(b_loaded, 16)
            for dst, src, loaded in ((wv_raw, Wv, wvm_loaded), (wmT_raw, WmT, wvm_loaded)):
                sp.dma_start(dst, src.rearrange("(k p) d -> p k d", p=P)).then_inc(loaded, 16)

            def load_group(g):
                sp.dma_start(val_in, valueT_v[:, :, bass.ds(g * GW, GW)]).then_inc(val_loaded, 16)
                sp.dma_start(x_in, x_groups[:, bass.ds(g * GT, GT), :]).then_inc(x_loaded, 16)
                sp.dma_start(key_in, keyT_v[:, :, bass.ds(g * GW, GW)]).then_inc(key_loaded, 16)

            load_group(0)
            with sp.Fori(0, G - 1) as g:
                sp.wait_ge(val_lo, g + 1)
                sp.dma_start(val_in, valueT_v[:, :, bass.ds(g * GW + GW, GW)]).then_inc(val_loaded, 16)
                sp.wait_ge(xnT_mm, g * GT + GT)
                sp.wait_ge(r_done, g * GT + GT)
                sp.dma_start(x_in, x_groups[:, bass.ds(g * GT + GT, GT), :]).then_inc(x_loaded, 16)
                sp.wait_ge(key_lo, g + 1)
                sp.dma_start(key_in, keyT_v[:, :, bass.ds(g * GW + GW, GW)]).then_inc(key_loaded, 16)
                sp.wait_ge(proj_lo, g * 8 + 8)
                sp.dma_start(q_dram[bass.ds(g * GT, GT)].rearrange("t p f -> p t f"),
                             q_out.rearrange("p t h k n -> p t (h k n)")).then_inc(q_stored, 16)
            sp.wait_ge(q_stored, 16 * (G - 1))
            sp.dma_start(q_in1, q_dram[1]).then_inc(q1_loaded, 16)
            sp.wait_ge(xnT_mm, G * GT)
            sp.wait_ge(r_done, G * GT)
            sp.dma_start(q_in, q_dram[0]).then_inc(q_loaded, 16)
            for c in range(C):
                if c == C // 2:
                    sp.wait_ge(proj_mm, G * 8 - 4)
                sp.dma_start(adj_in[:, c, :], adj_tiles[0, :, c * CW:(c + 1) * CW]).then_inc(adj_loaded[c], 16)
            sp.wait_ge(proj_lo, G * 8)
            sp.dma_start(q_dram[T - GT:T].rearrange("t p f -> p t f"),
                         q_out.rearrange("p t h k n -> p t (h k n)")).then_inc(q_stored, 16)
            sp.wait_ge(q_stored, 16 * G)
            sp.dma_start(x_res, x_tiles[0]).then_inc(xres_loaded, 16)
            sp.wait_ge(pads_ready, 5)
            for h in range(HALVES):
                sp.dma_start(outs[h][NH:NH + P, :], pad_row[:, 0:D]).then_inc(out_pads, 16)
                sp.dma_start(slots[h][DUMMY * P:(DUMMY + 1) * P, :], pad_row[:, :]).then_inc(out_pads, 16)

            def residual_io(t, h):
                sp.wait_ge(x1_done, t + 1)
                sp.dma_start(x_res, x_tiles[t + 1]).then_inc(xres_loaded, 16)
                sp.dma_start(out_tiles[h][t - h * TH], x1_out).then_inc(x1_stored, 16)

            def adjacency(t):
                for c in range(C):
                    sp.wait_ge(s_read, t * C - C + c + 1)
                    sp.dma_start(adj_in[:, c, :], adj_tiles[t, :, c * CW:(c + 1) * CW]).then_inc(adj_loaded[c], 16)

            def attend_io(t):
                adjacency(t)
                sp.wait_ge(s_mm, t * C)
                sp.dma_start(q_in, q_dram[t]).then_inc(q_loaded, 16)

            def pad_regions(h, experts=range(E)):
                sp.wait_ge(tables_done, h + 1)
                sp.wait_ge(slotted, 32 * TH * (h + 1))
                for e in experts:
                    at = sp.value_load(pad_at[0:1, h, e:e + 1], min_val=0, max_val=(DUMMY - 1) * P)
                    sp.dma_start(slots[h][bass.ds(at, P), :], pad_row[:, :]).then_inc(padded[h], 16)

            adjacency(1)
            with sp.Fori(2, TH + 2) as t:
                attend_io(t)
                residual_io(t - 2, 0)
            attend_io(TH + 2)
            residual_io(TH, 1)
            pad_regions(0)
            with sp.Fori(TH + 3, T) as t:
                attend_io(t)
                residual_io(t - 2, 1)
            sp.wait_ge(s_read, T * C)
            for e in range(2):
                sp.dma_start(we_in[:, e], weT_v[e]).then_inc(we_loaded[e], 16)
            residual_io(T - 2, 1)

            def load_block(st):
                if st.has(2):
                    sp.wait_ge(tokT_mm, st.count(2))
                    sp.wait_ge(tok_meta, st.count(2))
                at = sp.value_load(tab_row[0:1, st.h, bass.ds(st.k, 1)], min_val=0, max_val=DUMMY * P)
                sp.dma_start(tok_in[:, st.b2, :], slots[st.h][bass.ds(at, P), :]).then_inc(tok_loaded[st.b2], 16)

            lead = lead_steps()
            sp.wait_ge(padded[0], 16 * E)
            sp.wait_ge(out_pads, 32 * HALVES)
            sp.wait_ge(bias_done, T)
            for st in lead[:2]:
                load_block(st)
            sp.wait_ge(exp_done, T * C)
            sp.dma_start(be_all, be.rearrange("(a e) d -> a e d", a=1).to_broadcast([P, E, D])).then_inc(be_loaded, 16)
            for i, st in enumerate(lead[2:]):
                load_block(st)
                if i == 0:
                    sp.wait_ge(x1_done, T)
                    sp.dma_start(out_tiles[1][TH - 1], x1_out).then_inc(x1_stored, 16)
                if i + 2 in PADS_AFTER:
                    pad_regions(1, PADS_AFTER[i + 2])
            sp.wait_ge(padded[1], 16 * E)
            with sp.Fori(0, TURNS) as j:
                for st in turn_steps(j):
                    load_block(st)
            for st in tail_steps():
                load_block(st)
            for b in range(RING):
                sp.wait_ge(y_added[b], 16 * len(range(b, 2 * BLOCKS, RING)))

        @block.gpsimd
        def _(pool):
            nc.gpsimd.memset(ident[:, :], 0.0).then_inc(ident_step, 1)
            pool.wait_ge(ident_step, 1)
            nc.gpsimd.affine_select(out=ident[:, :], in_=ident[:, :], compare_op=ALU.not_equal, fill=1.0, base=0,
                                    pattern=[[-1, P]], channel_multiplier=1).then_inc(consts_ready, 1)
            for e in range(E):
                last = nc.gpsimd.memset(iota_e[:, e:e + 1], float(e))
            last.then_inc(consts_ready, 1)
            nc.gpsimd.memset(neg_half[:, :], -0.5).then_inc(ident_step, 1)
            pool.wait_ge(ident_step, 2)
            nc.gpsimd.memset(tri[:, :], 1.0).then_inc(ident_step, 1)
            nc.gpsimd.memset(pad_row[:, :], 0.0).then_inc(ident_step, 1)
            pool.wait_ge(ident_step, 4)
            nc.gpsimd.affine_select(out=tri[:, :], in_=tri[:, :], compare_op=ALU.is_gt, fill=0.0, base=0,
                                    pattern=[[1, P]], channel_multiplier=-1).then_inc(pads_ready, 1)
            for dst, step, n, base, per_row in ((pad_row[:, D:D + 1], 0, 1, NH, 1), (row_ids[:, :], P, TH, 0, 1),
                                                (iota_k[:, :], 1, BLOCKS, 0, 0), (region_start[:, :], REGION * P, E, 0, 0)):
                nc.gpsimd.iota(dst, pattern=[[step, n]], base=base, channel_multiplier=per_row,
                               allow_small_or_imprecise_dtypes=True).then_inc(pads_ready, 1)
            with pool.Fori(0, G) as g:
                pool.wait_ge(var_done, g + 1)
                nc.gpsimd.tensor_tensor(rstd[:, :], var_eps[:, :], neg_half[:, :], ALU.pow).then_inc(rstd_done, 1)
            def settle():
                pool.sem_inc(wait_passed_pool, 1)

            def inverse_deviation(t):
                pool.wait_ge(yvar_done, t + 1)
                settle()
                nc.gpsimd.tensor_tensor(rstd[:, 0:1], var_eps[:, 0:1], neg_half[:, 0:1], ALU.pow).then_inc(yrstd_done, 1)

            def scatter_rows(t, h):
                pool.wait_ge(slot_step, t * SLOT_STEPS + SLOT_STEPS)
                settle()
                for i in range(2):
                    nc.gpsimd.tensor_copy(row_buf[:, D + 1:D + 2], gate[:, i:i + 1]).then_inc(gate_put, 1)
                    pool.wait_ge(gate_put, t * 2 + i + 1)
                    settle()
                    nc.gpsimd.indirect_dma_start(
                        out=slots[h], out_offset=bass.IndirectOffsetOnAxis(ap=slots_u[:, i:i + 1], axis=0),
                        in_=row_buf, in_offset=None).then_inc(slotted, 16)
                    pool.wait_ge(slotted, t * 32 + i * 16 + 16)
                    settle()

            pool.wait_ge(out_pads, 32 * HALVES)
            with pool.Fori(0, TH) as t:
                inverse_deviation(t)
                scatter_rows(t, 0)
            with pool.Fori(TH, T - 1) as t:
                inverse_deviation(t)
                scatter_rows(t, 1)
            inverse_deviation(T - 1)

            def add_block(st):
                pool.wait_ge(y_scaled, st.count())
                back = 1 if st.alone else 2
                if st.has(back):
                    pool.wait_ge(y_added[(st.base - back) % RING], st.uses(RING, back) * 16)
                settle()
                nc.gpsimd.indirect_dma_start(
                    out=outs[st.h], out_offset=bass.IndirectOffsetOnAxis(ap=tok_ids[:, st.b4:st.b4 + 1], axis=0),
                    in_=y_out[:, st.b4, :], in_offset=None, compute_op=ALU.add).then_inc(y_added[st.b4], 16)

            pool.wait_ge(x1_stored, 16 * T)
            for st in lead_steps():
                if st.k == 3:
                    scatter_rows(T - 1, 1)
                add_block(st)
            pool.wait_ge(y_added[(LEAD - 1) % RING], 16 * ((LEAD - 1) // RING + 1))
            with pool.Fori(0, TURNS) as j:
                for st in turn_steps(j):
                    add_block(st)
            for st in tail_steps():
                add_block(st)

        @block.scalar
        def _(act):
            for i in range(2 * KC):
                act.wait_ge(fold_mm, i + 1)
                dst = (foldA if i < KC else foldV)[:, 0, i % KC, :]
                nc.scalar.activation(dst, ps[:, i, :], ACT.Copy, scale=WS).then_inc(fold_hi, 1)

            def split_values(g):
                act.wait_ge(val_loaded, g * 16 + 16)
                if not is0(g):
                    act.wait_ge(proj_mm, g * 8 - 4)
                nc.scalar.activation(vT[:, 0], val_in, ACT.Copy).then_inc(val_hi, 1)

            def project(g, last=False):
                def turned(s):
                    act.wait_ge(xnT_mm, g * GT + s + 1)
                    if s == 0 and not is0(g):
                        act.wait_ge(proj_mm, g * 8)
                    nc.scalar.activation(xnT[:, 0, :, s * P:(s + 1) * P],
                                         tr_bank(s).rearrange("p (k n) -> p k n", k=KC), ACT.Copy).then_inc(xnT_hi, 1)

                for s in range(GT):
                    act.wait_ge(proj_mm, g * 8 + s + 1)
                    nc.scalar.activation(v[:, 0, g * GT + s, :], mm_bank(s), ACT.Copy).then_inc(proj_hi, 1)
                    for turn in TURNS_AFTER[s]:
                        turned(turn)
                if not last:
                    split_values(g + 1)
                for j in range(KC):
                    if j == (0 if last else 1):
                        act.wait_ge(key_loaded, g * 16 + 16)
                        nc.scalar.activation(kT[:, 0, :, bass.ds(g * GW, GW)], key_in, ACT.Copy).then_inc(key_hi, 1)
                    act.wait_ge(proj_mm, g * 8 + 4 + j + 1)
                    if j == 0 and not is0(g):
                        act.wait_ge(q_stored, g * 16)
                    nc.scalar.activation(q_out[:, :, 0, j, :], mm_bank(j).rearrange("p (t n) -> p t n", t=GT),
                                         ACT.Identity, bias=u_col[:, j:j + 1]).then_inc(proj_hi, 1)

            split_values(0)
            act.wait_ge(fold_out, 2 * KC + 3)
            project(0)
            with act.Fori(1, G - 1) as g:
                project(g)
            project(G - 1, last=True)

            def absolute(t, c):
                act.wait_ge(s_read, t * C + c + 1)
                if not (is0(t) and c < 2):
                    act.wait_ge(w_done, t * C + c - 1)
                nc.scalar.activation(s_abs[:, c % 2, :], s_adj[:, c % 2, :], ACT.Abs).then_inc(abs_done, 1)

            def exponent(t, c):
                if c == 0:
                    act.wait_ge(bias_done, t + 1)
                if not is0(t):
                    act.wait_ge(pT_mm, t * C - C + c + 1)
                nc.scalar.activation(prob[:, c * CW:(c + 1) * CW], w[:, c * CW:(c + 1) * CW], ACT.Exp,
                                     bias=exp_bias[:, :], scale=1.0 / SS,
                                     accum_out=sum_part[:, c:c + 1]).then_inc(exp_done, 1)

            def high_half(t, c):
                act.wait_ge(pT_mm, t * C + c + 1)
                if not (is0(t) and c < 2):
                    act.wait_ge(pv_mm, t * C + c - 1)
                nc.scalar.activation(pT[:, c % 2, 0], pT_bank(c).rearrange("p (m n) -> p m n", m=MT),
                                     ACT.Copy).then_inc(pT_hi, 1)

            for c in range(C):
                absolute(0, c)
            act.wait_ge(q_stored, G * 16)

            def attend(t, routes):
                for c in range(4):
                    exponent(t - 1, c)
                absolute(t, 0)
                for c in range(4, 6):
                    exponent(t - 1, c)
                absolute(t, 1)
                for c in range(6, C):
                    exponent(t - 1, c)
                for c in range(C):
                    high_half(t - 1, c)
                    if c + 2 < C:
                        absolute(t, c + 2)
                    if c == 3 and routes:
                        copy_turned(t - 2)
                    if c == 5 and routes:
                        gap_exponent(t - 2)

            def copy_turned(t):
                act.wait_ge(ynT_mm, t + 1)
                if not is0(t):
                    act.wait_ge(gate_mm, t)
                nc.scalar.activation(ynT32, ynT_bank.rearrange("p (k n) -> p k n", k=KC), ACT.Copy).then_inc(ynT_act, 1)

            def gap_exponent(t):
                act.wait_ge(gate_step, t * GATE_STEPS + 5)
                nc.scalar.activation(egap[:, :], gap[:, :], ACT.Exp).then_inc(egap_done, 1)

            attend(1, False)
            with act.Fori(2, T) as t:
                attend(t, True)

            def expert_hi(n):
                e, ks = n // 2, halves_of_k[n % 2]
                if n % 2 == 0 and 0 < e < E - 1:
                    act.wait_ge(we_lo, n)
                    nc.scalar.dma_start(we_in[:, (e + 1) % 2], weT_v[e + 1]).then_inc(we_loaded[(e + 1) % 2], 16)
                act.wait_ge(we_loaded[e % 2], 16 * (e // 2 + 1))
                nc.scalar.activation(we[:, 0, e, ks], we_in[:, e % 2, ks], ACT.Copy, scale=WS).then_inc(we_hi, 1)

            exponent(T - 1, 0)
            exponent(T - 1, 1)
            for c in range(C):
                high_half(T - 1, c)
                if c + 2 < C:
                    exponent(T - 1, c + 2)
                if c == 3:
                    copy_turned(T - 2)
                if c == 5:
                    gap_exponent(T - 2)
                expert_hi(c)

            def block_hi(st):
                act.wait_ge(tokT_mm, st.count())
                if st.has(2):
                    act.wait_ge(y_mm, st.count(2))
                nc.scalar.activation(tokT[:, st.b2, 0], tokT_bank(st.b2).rearrange("p (k n) -> p k n", k=KC),
                                     ACT.Copy).then_inc(tokT_hi, 1)

            def block_gate(st):
                act.wait_ge(y_biased, st.count())
                if st.has(RING):
                    act.wait_ge(y_added[st.b4], st.uses(RING, RING) * 16)
                nc.scalar.activation(y_out[:, st.b4, :], y_tmp[:, st.b2, :], ACT.Copy,
                                     scale=tok_gates[:, st.b4:st.b4 + 1]).then_inc(y_scaled, 1)

            lead = lead_steps()
            block_hi(lead[0])
            for i, st in enumerate(lead):
                block_hi((lead + turn_steps(0))[i + 1])
                if SPLIT_EARLY + i < 2 * E:
                    expert_hi(SPLIT_EARLY + i)
                block_gate(st)
                if i == 1:
                    copy_turned(T - 1)
                if i == 2:
                    gap_exponent(T - 1)
            with act.Fori(0, TURNS) as j:
                steps = turn_steps(j) + turn_steps(j + 1)[:1]
                for st, after in zip(steps, steps[1:]):
                    block_hi(after)
                    block_gate(st)
            tail = tail_steps()
            for i, st in enumerate(tail):
                if i + 1 < LEAD:
                    block_hi(tail[i + 1])
                block_gate(st)

        @block.vector
        def _(dve):
            def settle():
                dve.sem_inc(wait_passed, 1)

            nc.vector.memset(ones[:, :], 1.0).then_inc(ones_ready, 1)
            dve.wait_ge(ones_ready, 1)
            dve.wait_ge(b_loaded, 16 * 6)
            for i, col in ((0, bk_col), (1, bv_col)):
                for k in range(KC):
                    last = nc.vector.tensor_scalar(x_wide[i][:, k, :], ones[:, :], col[:, k:k + 1], None, ALU.mult)
            last.then_inc(bias_cols_wide, 1)
            def split_values(g):
                dve.wait_ge(val_hi, g + 1)
                nc.vector.tensor_tensor(vT[:, 1], val_in, vT[:, 0], ALU.subtract).then_inc(val_lo, 1)

            for i in range(2 * KC):
                dve.wait_ge(fold_hi, i + 1)
                f = foldA if i < KC else foldV
                nc.vector.scalar_tensor_tensor(f[:, 1, i % KC, :], ps[:, i, :], WS, f[:, 0, i % KC, :],
                                               ALU.mult, ALU.subtract).then_inc(fold_out, 1)
            split_values(0)
            dve.wait_ge(fold_mm, 2 * KC + 1)
            nc.vector.tensor_scalar(g_row, ps[:, 0, :], WS, None, ALU.mult).then_inc(fold_out, 1)
            dve.wait_ge(fold_mm, 2 * KC + 2)
            nc.vector.tensor_copy(c_row[:, :], ps[:, 1, :]).then_inc(fold_out, 1)
            dve.wait_ge(fold_mm, 2 * KC + 3)
            nc.vector.tensor_scalar(u_col[:, :], ps[:, 2, 0:KC], WS, None, ALU.mult)
            nc.vector.tensor_scalar(c0[:, :], ps[:, 2, KC:KC + 1], WS, None, ALU.mult).then_inc(fold_out, 1)
            dve.wait_ge(fold_out, 2 * KC + 3)

            def spread(g):
                dve.wait_ge(x_loaded, g * 16 + 16)
                for s in range(GT):
                    last = nc.vector.bn_stats(stats[:, s, :], x_in[:, s, :])
                last.then_inc(stats_done, 1)
                dve.wait_ge(stats_done, g + 1)
                settle()
                for s in range(GT):
                    last = nc.vector.bn_aggr(moments[:, s, :], stats[:, s, :])
                last.then_inc(moments_done, 1)
                dve.wait_ge(moments_done, g + 1)
                nc.vector.tensor_scalar(var_eps[:, :], moments[:, :, 1], EPS, None, ALU.add).then_inc(var_done, 1)

            def normalize(g):
                dve.wait_ge(rstd_done, g + 1)
                for s in range(GT):
                    nc.vector.tensor_scalar(x_in[:, s, :], x_in[:, s, :], moments[:, s, 0:1], rstd[:, s:s + 1],
                                            ALU.subtract, ALU.mult).then_inc(xn_done, 1)

            def project(g, last=False):
                def turned(s):
                    dve.wait_ge(xnT_hi, g * GT + s + 1)
                    nc.vector.tensor_tensor(xnT[:, 1, :, s * P:(s + 1) * P],
                                            tr_bank(s).rearrange("p (k n) -> p k n", k=KC),
                                            xnT[:, 0, :, s * P:(s + 1) * P], ALU.subtract).then_inc(xnT_lo, 1)

                def key_bias(s):
                    dve.wait_ge(xn_done, g * GT + s + 1)
                    if not (is0(g) and s == 0):
                        dve.wait_ge(r_done, g * GT + s)
                    settle()
                    nc.vector.tensor_tensor_reduce(out=r_junk, in0=x_in[:, s, :], in1=g_row, scale=1.0,
                                                   scalar=c0[:, :], op0=ALU.mult, op1=ALU.add,
                                                   accum_out=r_tmp[:, s:s + 1]).then_inc(r_done, 1)

                for s in range(GT):
                    dve.wait_ge(proj_hi, g * 8 + s + 1)
                    nc.vector.tensor_tensor(v[:, 1, g * GT + s, :], mm_bank(s), v[:, 0, g * GT + s, :],
                                            ALU.subtract).then_inc(proj_lo, 1)
                    for turn in TURNS_AFTER[s]:
                        turned(turn)
                    for turn in TURNS_AFTER[s]:
                        key_bias(turn)
                dve.wait_ge(r_done, g * GT + GT)
                nc.vector.tensor_copy(r_all[:, bass.ds(g * GT, GT)], r_tmp[:, :]).then_inc(r_kept, 1)
                for j in range(KC):
                    dve.wait_ge(proj_hi, g * 8 + 4 + j + 1)
                    nc.vector.scalar_tensor_tensor(q_out[:, :, 1, j, :],
                                                   mm_bank(j).rearrange("p (t n) -> p t n", t=GT),
                                                   u_col[:, j:j + 1], q_out[:, :, 0, j, :],
                                                   ALU.add, ALU.subtract).then_inc(proj_lo, 1)
                    if j == 0 and not last:
                        split_values(g + 1)
                    if j == (0 if last else 1):
                        dve.wait_ge(key_hi, g + 1)
                        nc.vector.tensor_tensor(kT[:, 1, :, bass.ds(g * GW, GW)], key_in,
                                                kT[:, 0, :, bass.ds(g * GW, GW)], ALU.subtract).then_inc(key_lo, 1)
                    if j == 2 and not last:
                        spread(g + 1)
                if not last:
                    normalize(g + 1)

            spread(0)
            normalize(0)
            project(0)
            with dve.Fori(1, G - 1) as g:
                project(g)
            project(G - 1, last=True)
            dve.wait_ge(r_kept, G)

            def row_consts(t):
                nc.vector.tensor_copy(r_cur[:, :], r_all[:, bass.ds(t, 1)]).then_inc(rcur_done, 1)
                dve.wait_ge(rcur_done, t + 1)

            def times_adj(t, c):
                dve.wait_ge(s_mm, t * C + c + 1)
                dve.wait_ge(adj_loaded[c], t * 16 + 16)
                nc.vector.scalar_tensor_tensor(s_adj[:, c % 2, :], s_bank(c), r_cur[:, :], adj_in[:, c, :],
                                               ALU.add, ALU.mult).then_inc(s_read, 1)

            def mask(t, c):
                dve.wait_ge(abs_done, t * C + c + 1)
                nc.vector.tensor_scalar(s_abs[:, c % 2, :], s_abs[:, c % 2, :], THRESHOLD * SS, NEG * SS,
                                        ALU.is_lt, ALU.mult).then_inc(mask_done, 1)
                dve.wait_ge(mask_done, t * C + c + 1)
                if not is0(t):
                    dve.wait_ge(exp_done, t * C - C + c + 1)
                settle()
                nc.vector.tensor_tensor_reduce(out=w[:, c * CW:(c + 1) * CW], in0=s_adj[:, c % 2, :],
                                               in1=s_abs[:, c % 2, :], scale=1.0, scalar=-3.0e38,
                                               op0=ALU.add, op1=ALU.max,
                                               accum_out=max_part[:, c:c + 1]).then_inc(w_done, 1)

            def softmax_bias(t):
                dve.wait_ge(w_done, t * C + C)
                nc.vector.reduce_max(row_max[:, :], max_part[:, :], AX_X).then_inc(max_done, 1)
                dve.wait_ge(max_done, t + 1)
                nc.vector.tensor_scalar(exp_bias[:, :], row_max[:, :], -1.0 / SS, None, ALU.mult).then_inc(bias_done, 1)

            def low_half(t, c):
                dve.wait_ge(pT_hi, t * C + c + 1)
                nc.vector.tensor_tensor(pT[:, c % 2, 1], pT_bank(c).rearrange("p (m n) -> p m n", m=MT),
                                        pT[:, c % 2, 0], ALU.subtract).then_inc(pT_lo, 1)

            def inverse_sum(t):
                dve.wait_ge(exp_done, t * C + C)
                nc.vector.reduce_sum(row_sum[:, :], sum_part[:, :], AX_X).then_inc(sum_done, 1)
                dve.wait_ge(sum_done, t + 1)
                nc.vector.tensor_scalar(row_sum_ws[:, :], row_sum[:, :], WS, None, ALU.mult).then_inc(sum_ws_done, 1)
                dve.wait_ge(sum_ws_done, t + 1)
                nc.vector.reciprocal(inv_sum[:, :], row_sum_ws[:, :]).then_inc(inv_done, 1)
                dve.wait_ge(xres_loaded, t * 16 + 16)
                nc.vector.tensor_tensor(x_res, x_res, c_row[:, :], ALU.add).then_inc(xc_done, 1)

            def residual(t):
                dve.wait_ge(xc_done, t + 1)
                dve.wait_ge(inv_done, t + 1)
                dve.wait_ge(pv_mm, t * C + C)
                if not is0(t):
                    dve.wait_ge(x1_stored, t * 16)
                nc.vector.scalar_tensor_tensor(x1_out, o_bank, inv_sum[:, :], x_res, ALU.mult,
                                               ALU.add).then_inc(x1_done, 1)

            row_consts(0)
            for c in range(C):
                times_adj(0, c)
                mask(0, c)
            softmax_bias(0)
            dve.wait_ge(q_stored, G * 16)
            def route_stats(t):
                dve.wait_ge(x1_done, t + 1)
                nc.vector.bn_stats(stats[:, 0, :], x1_out).then_inc(ystats_done, 1)
                dve.wait_ge(ystats_done, t + 1)
                settle()
                nc.vector.bn_aggr(moments[:, 0, :], stats[:, 0, :]).then_inc(ymom_done, 1)
                dve.wait_ge(ymom_done, t + 1)
                nc.vector.tensor_scalar(var_eps[:, 0:1], moments[:, 0, 1:2], EPS, None, ALU.add).then_inc(yvar_done, 1)

            def route_rows(t, h):
                if not is0(t):
                    dve.wait_ge(slotted, t * 32)
                nc.vector.tensor_copy(row_buf[:, D:D + 1], row_ids[:, bass.ds(t - h * TH, 1)])
                dve.wait_ge(yrstd_done, t + 1)
                nc.vector.tensor_scalar(row_buf[:, 0:D], x1_out, moments[:, 0, 0:1], rstd[:, 0:1],
                                        ALU.subtract, ALU.mult).then_inc(yn_done, 1)

            def stepper(done, t, per_tile, first=0):
                n = [first]

                def step(ins):
                    n[0] += 1
                    ins.then_inc(done, 1)
                    dve.wait_ge(done, t * per_tile + n[0])
                return step

            def route_top2(t):
                step = stepper(gate_step, t, GATE_STEPS)
                dve.wait_ge(gate_mm, t + 1)
                step(nc.vector.tensor_copy(logits[:, :], gate_bank))
                settle()
                step(nc.vector.max(top8[:, :], logits[:, :]))
                settle()
                step(nc.vector.max_index(top_idx[:, :], top8[:, :], logits[:, :]))
                step(nc.vector.tensor_copy(top_idx_f[:, :], top_idx[:, :]))
                step(nc.vector.tensor_tensor(gap[:, :], top8[:, 1:2], top8[:, 0:1], ALU.subtract))

            def route_gates(t):
                step = stepper(gate_step, t, GATE_STEPS, 5)
                dve.wait_ge(egap_done, t + 1)
                step(nc.vector.tensor_scalar(den[:, :], egap[:, :], 1.0, None, ALU.add))
                step(nc.vector.reciprocal(gate[:, 0:1], den[:, :]))
                step(nc.vector.tensor_tensor(gate[:, 1:2], gate[:, 0:1], egap[:, :], ALU.mult))
                step = stepper(pick_step, t, PICK_STEPS)
                nc.vector.tensor_scalar(pick[:, 0, :], iota_e[:, :], top_idx_f[:, 0:1], None, ALU.is_equal)
                step(nc.vector.tensor_scalar(pick[:, 1, :], iota_e[:, :], top_idx_f[:, 1:2], None, ALU.is_equal))
                step(nc.vector.tensor_tensor(picked[:, :], pick[:, 0, :], pick[:, 1, :], ALU.add))

            def route_slots(t):
                step = stepper(slot_step, t, SLOT_STEPS)
                dve.wait_ge(rank_mm, t + 1)
                step(nc.vector.tensor_tensor(slot_of[:, :], rank_bank, next_slot[:, :], ALU.add))
                for i in range(2):
                    step(nc.vector.tensor_tensor_reduce(out=slot_junk[:, :], in0=pick[:, i, :], in1=slot_of[:, :],
                                                        scale=1.0, scalar=0.0, op0=ALU.mult, op1=ALU.add,
                                                        accum_out=slots_f[:, i:i + 1]))
                step(nc.vector.tensor_tensor(next_slot[:, :], count_bank, next_slot[:, :], ALU.add))
                step(nc.vector.tensor_copy(slots_u[:, :], slots_f[:, :]))

            def tables(h):
                n = [0]

                def step(ins):
                    n[0] += 1
                    ins.then_inc(tables_step, 1)
                    dve.wait_ge(tables_step, h * TABLE_STEPS + n[0])

                row0 = slice(0, 1)
                nc.vector.tensor_copy(pad_at[row0, h, :], next_slot[row0, :])
                step(nc.vector.scalar_tensor_tensor(blocks_u[:, :], next_slot[row0, :], float(P - 1),
                                                    region_start[row0, :], ALU.add, ALU.subtract))
                step(nc.vector.tensor_scalar(blocks_u[:, :], blocks_u[:, :], 7, None, ALU.logical_shift_right))
                Z = E // 2
                for i in range(2):
                    nc.vector.memset(blocks_f[i][:, 0:Z], 0.0)
                step(nc.vector.tensor_copy(blocks_f[0][:, Z:], blocks_u[:, :]))
                nc.vector.tensor_scalar(region_gap[:, :], blocks_f[0][:, Z:], -1.0, float(REGION), ALU.mult, ALU.add)
                for i, back in enumerate((1, 2, 4)):
                    src, dst = blocks_f[i % 2], blocks_f[(i + 1) % 2]
                    step(nc.vector.tensor_tensor(dst[:, Z:], src[:, Z:], src[:, Z - back:Z - back + E], ALU.add))
                per_step = lambda row: row.rearrange("p (a e) -> p a e", a=1).to_broadcast([1, BLOCKS, E])
                step(nc.vector.tensor_tensor(behind[:, :, :],
                                             iota_k[:, :].rearrange("p (b a) -> p b a", a=1).to_broadcast([1, BLOCKS, E]),
                                             per_step(blocks_f[1][:, Z:]), ALU.is_ge))
                step(nc.vector.reduce_sum(tab_f[:, 1, :], behind[:, :, :], AX_X))
                step(nc.vector.tensor_tensor(behind[:, :, :], behind[:, :, :], per_step(region_gap[:, :]), ALU.mult))
                step(nc.vector.reduce_sum(tab_f[:, 0, :], behind[:, :, :], AX_X))
                step(nc.vector.tensor_tensor(tab_f[:, 0, :], tab_f[:, 0, :], iota_k[:, :], ALU.add))
                assert n[0] == TABLE_STEPS, n[0]
                nc.vector.tensor_scalar(tab_row[:, h, :], tab_f[:, 0, :], float(DUMMY), float(P), ALU.min, ALU.mult)
                nc.vector.tensor_scalar(tab_expert[:, h, :], tab_f[:, 1, :], float(E - 1), None, ALU.min
                                        ).then_inc(tables_done, 1)

            def first_slots(h):
                if h:
                    dve.wait_ge(tables_done, h)
                nc.vector.tensor_copy(next_slot[:, :], region_start[:, :]).then_inc(slots_reset, 1)
                dve.wait_ge(slots_reset, h + 1)

            def attend(t, h=None):
                if h is not None:
                    route_stats(t - 2)
                row_consts(t)
                times_adj(t, 0)
                times_adj(t, 1)
                for c in range(C):
                    if c == 0:
                        mask(t, 0)
                    elif c + 1 < C:
                        mask(t, c + 1)
                    if c == 2:
                        inverse_sum(t - 1)
                        if h is not None:
                            route_rows(t - 2, h)
                    if c == C - 2:
                        softmax_bias(t)
                    low_half(t - 1, c)
                    if c == 0:
                        mask(t, 1)
                    if c + 2 < C:
                        times_adj(t, c + 2)
                    if h is not None:
                        if c == 5:
                            route_top2(t - 2)
                        if c == 6:
                            route_gates(t - 2)
                        if c == 7:
                            route_slots(t - 2)
                residual(t - 1)

            attend(1)
            dve.wait_ge(pads_ready, 5)
            first_slots(0)
            with dve.Fori(2, TH + 2) as t:
                attend(t, 0)
            tables(0)
            first_slots(1)
            with dve.Fori(TH + 2, T) as t:
                attend(t, 1)

            def expert_lo(n):
                e, ks = n // 2, halves_of_k[n % 2]
                dve.wait_ge(we_hi, n + 1)
                nc.vector.scalar_tensor_tensor(we[:, 1, e, ks].rearrange("p k o -> p (k o)"),
                                               we_in[:, e % 2, ks].rearrange("p k o -> p (k o)"), WS,
                                               we[:, 0, e, ks].rearrange("p k o -> p (k o)"),
                                               ALU.mult, ALU.subtract).then_inc(we_lo, 1)

            route_stats(T - 2)
            for c in range(C):
                low_half(T - 1, c)
                if c == 6:
                    inverse_sum(T - 1)
                if c == 2:
                    route_rows(T - 2, 1)
                if c == 5:
                    route_top2(T - 2)
                if c == 6:
                    route_gates(T - 2)
                if c == 7:
                    route_slots(T - 2)
                expert_lo(c)

            def block_lo(st):
                dve.wait_ge(tok_loaded[st.b2], st.uses(2) * 16)
                if st.has(RING):
                    dve.wait_ge(y_added[st.b4], st.uses(RING, RING) * 16)
                nc.vector.tensor_copy(tok_ids[:, st.b4:st.b4 + 1], tok_in[:, st.b2, D:D + 1])
                nc.vector.tensor_copy(tok_gates[:, st.b4:st.b4 + 1], tok_in[:, st.b2, D + 1:D + 2]).then_inc(tok_meta, 1)
                dve.wait_ge(tokT_hi, st.count())
                nc.vector.tensor_tensor(tokT[:, st.b2, 1], tokT_bank(st.b2).rearrange("p (k n) -> p k n", k=KC),
                                        tokT[:, st.b2, 0], ALU.subtract).then_inc(tokT_lo, 1)

            def block_bias(st):
                e = dve.value_load(tab_expert[0:1, st.h, bass.ds(st.k, 1)], min_val=0, max_val=E - 1)
                dve.wait_ge(y_mm, st.count())
                if st.has(2):
                    dve.wait_ge(y_scaled, st.count(2))
                nc.vector.scalar_tensor_tensor(y_tmp[:, st.b2, :], y_bank(st.b2), 1.0 / WS, be_all[:, e, :],
                                               ALU.mult, ALU.add).then_inc(y_biased, 1)

            lead = lead_steps()
            block_lo(lead[0])
            residual(T - 1)
            route_stats(T - 1)
            dve.wait_ge(be_loaded, 16)
            dve.wait_ge(tables_done, 1)
            for i, st in enumerate(lead):
                block_lo((lead + turn_steps(0))[i + 1])
                if SPLIT_EARLY + i < 2 * E:
                    expert_lo(SPLIT_EARLY + i)
                if i == 0:
                    route_rows(T - 1, 1)
                block_bias(st)
                if i == 2:
                    route_top2(T - 1)
                    route_gates(T - 1)
                if i == 3:
                    route_slots(T - 1)
                    tables(1)
            dve.wait_ge(tables_done, 2)
            with dve.Fori(0, TURNS) as j:
                steps = turn_steps(j) + turn_steps(j + 1)[:1]
                for st, after in zip(steps, steps[1:]):
                    block_lo(after)
                    block_bias(st)
            tail = tail_steps()
            for i, st in enumerate(tail):
                if i + 1 < LEAD:
                    block_lo(tail[i + 1])
                block_bias(st)

        @block.tensor
        def _(pe):
            def product(bank, pairs):
                n = len(pairs)
                for k, (st, mv) in enumerate(pairs):
                    nc.tensor.matmul(bank, st[0], mv[0], start=(k == 0), stop=False)
                    nc.tensor.matmul(bank, st[0], mv[1], start=False, stop=False)
                    last = nc.tensor.matmul(bank, st[1], mv[0], start=False, stop=(k == n - 1))
                return last

            def exact(bank, pairs):
                n = len(pairs)
                for k, (st, mv) in enumerate(pairs):
                    last = nc.tensor.matmul(bank, st, mv, start=(k == 0), stop=(k == n - 1))
                return last

            for o in range(KC):
                pe.wait_ge(wqk_loaded[o], 32)
                for i in range(KC):
                    last = nc.tensor.matmul(ps[:, i, :], wq_raw[:, o, i * P:(i + 1) * P], wk_raw[:, o, :],
                                            start=(o == 0), stop=(o == KC - 1))
                    if o == KC - 1:
                        last.then_inc(fold_mm, 1)
            pe.wait_ge(wvm_loaded, 32)
            for i in range(KC):
                exact(ps[:, KC + i, :], [(wv_raw[:, o, i * P:(i + 1) * P], wmT_raw[:, o, :])
                                         for o in range(KC)]).then_inc(fold_mm, 1)
            pe.wait_ge(bias_cols_wide, 1)
            pe.wait_ge(fold_out, 1)
            exact(ps[:, 0, :], [(x_wide[0][:, o, :], wq_raw[:, o, :]) for o in range(KC)]).then_inc(fold_mm, 1)
            pe.wait_ge(fold_out, 2)
            exact(ps[:, 1, :], [(x_wide[1][:, o, :], wmT_raw[:, o, :]) for o in range(KC)]
                  + [(ones[0:1, :], bm_row[:, :])]).then_inc(fold_mm, 1)
            pe.wait_ge(fold_out, 3)
            for j in range(KC):
                exact(ps[:, 2, j:j + 1], [(wk_raw[:, o, j * P:(j + 1) * P], bq_col[:, o:o + 1]) for o in range(KC)])
            exact(ps[:, 2, KC:KC + 1], [(x_wide[0][:, o, :], bq_col[:, o:o + 1])
                                        for o in range(KC)]).then_inc(fold_mm, 1)

            pe.wait_ge(fold_out, 2 * KC)
            pe.wait_ge(consts_ready, 2)

            def project(g):
                def turn(s):
                    pe.wait_ge(xn_done, g * GT + s + 1)
                    if not is0(g):
                        pe.wait_ge(xnT_lo, g * GT + s - 3)
                    elif s == 0:
                        pe.wait_ge(fold_out, 2 * KC + 3)
                    for k in range(KC):
                        last = nc.tensor.transpose(tr_bank(s)[:, k * P:(k + 1) * P],
                                                   x_in[:, s, k * P:(k + 1) * P], ident[:, :])
                    last.then_inc(xnT_mm, 1)

                for s in range(GT):
                    if s == 0:
                        pe.wait_ge(val_lo, g + 1)
                    if not is0(g):
                        pe.wait_ge(proj_lo, g * 8 - 4 + s + 1)
                    product(mm_bank(s), [((vT[:, 0, k, s * P:(s + 1) * P], vT[:, 1, k, s * P:(s + 1) * P]),
                                          (foldV[:, 0, k, :], foldV[:, 1, k, :])) for k in range(KC)]
                            ).then_inc(proj_mm, 1)
                    for tile in TURNS_AFTER[s]:
                        turn(tile)
                for j in range(KC):
                    if j == 0:
                        pe.wait_ge(xnT_lo, g * GT + GT)
                    pe.wait_ge(proj_lo, g * 8 + j + 1)
                    product(mm_bank(j), [((foldA[:, 0, k, j * P:(j + 1) * P], foldA[:, 1, k, j * P:(j + 1) * P]),
                                          (xnT[:, 0, k, :], xnT[:, 1, k, :])) for k in range(KC)]
                            ).then_inc(proj_mm, 1)

            project(0)
            with pe.Fori(1, G) as g:
                project(g)
            assert C == G and not C % 2

            def scores(t, c):
                q = q_in
                if is0(t):
                    pe.wait_ge(key_lo, c + 1)
                if isinstance(t, int) and t == 1:
                    q = q_in1
                    if c == 0:
                        pe.wait_ge(q1_loaded, 16)
                elif c == 0:
                    pe.wait_ge(q_loaded, 16 if is0(t) else t * 16)
                if not (is0(t) and c < 2):
                    pe.wait_ge(s_read, t * C + c - 1)
                product(s_bank(c), [((q[:, 0, k, :], q[:, 1, k, :]),
                                     (kT[:, 0, k, c * CW:(c + 1) * CW], kT[:, 1, k, c * CW:(c + 1) * CW]))
                                    for k in range(KC)]).then_inc(s_mm, 1)

            def turn_probs(t, c):
                pe.wait_ge(exp_done, t * C + c + 1)
                if not (is0(t) and c < 2):
                    pe.wait_ge(pT_lo, t * C + c - 1)
                for m in range(MT):
                    at = c * CW + m * P
                    last = nc.tensor.transpose(pT_bank(c)[:, m * P:(m + 1) * P], prob[:, at:at + P], ident[:, :])
                last.then_inc(pT_mm, 1)

            def times_values(t, c):
                pe.wait_ge(pT_lo, t * C + c + 1)
                if c == 0 and not is0(t):
                    pe.wait_ge(x1_done, t)
                for m in range(MT):
                    st = (pT[:, c % 2, 0, m, :], pT[:, c % 2, 1, m, :])
                    mv = (v[:, 0, c * MT + m, :], v[:, 1, c * MT + m, :])
                    first, final = c == 0 and m == 0, c == C - 1 and m == MT - 1
                    nc.tensor.matmul(o_bank, st[0], mv[0], start=first, stop=False)
                    nc.tensor.matmul(o_bank, st[0], mv[1], start=False, stop=False)
                    last = nc.tensor.matmul(o_bank, st[1], mv[0], start=False, stop=final)
                last.then_inc(pv_mm, 1)

            def turn_rows(t):
                pe.wait_ge(yn_done, t + 1)
                if not is0(t):
                    pe.wait_ge(ynT_act, t)
                for k in range(KC):
                    last = nc.tensor.transpose(ynT_bank[:, k * P:(k + 1) * P], row_buf[:, k * P:(k + 1) * P], ident[:, :])
                last.then_inc(ynT_mm, 1)

            def gate_logits(t):
                pe.wait_ge(ynT_act, t + 1)
                if not is0(t):
                    pe.wait_ge(slot_step, t * SLOT_STEPS)
                exact(gate_bank, [(ynT32[:, k, :], wg[:, k, :]) for k in range(KC)]
                      + [(ones[0:1, :], bg_row[:, :])]).then_inc(gate_mm, 1)

            def ranks(t):
                pe.wait_ge(pick_step, t * PICK_STEPS + PICK_STEPS)
                nc.tensor.matmul(rank_bank, tri[:, :], picked[:, :], start=True, stop=True)
                nc.tensor.matmul(count_bank, ones[:, :], picked[:, :], start=True, stop=True).then_inc(rank_mm, 1)

            def attend(t, routes):
                scores(t, 0)
                scores(t, 1)
                for c in range(C):
                    turn_probs(t - 1, c)
                    if c == 3 and routes:
                        turn_rows(t - 2)
                    if c + 2 < C:
                        scores(t, c + 2)
                    if c == 4 and routes:
                        gate_logits(t - 2)
                    if c >= 1:
                        times_values(t - 1, c - 1)
                times_values(t - 1, C - 1)
                if routes:
                    ranks(t - 2)

            for c in range(C):
                scores(0, c)
            pe.wait_ge(proj_lo, G * 8)
            attend(1, False)
            pe.wait_ge(pads_ready, 1)
            with pe.Fori(2, T) as t:
                attend(t, True)

            def turn_block(st):
                pe.wait_ge(tok_loaded[st.b2], st.uses(2) * 16)
                if st.has(2):
                    pe.wait_ge(tokT_lo, st.count(2))
                for k in range(KC):
                    last = nc.tensor.transpose(tokT_bank(st.b2)[:, k * P:(k + 1) * P],
                                               tok_in[:, st.b2, k * P:(k + 1) * P], ident[:, :])
                last.then_inc(tokT_mm, 1)

            def multiply_block(st, lead):
                e = pe.value_load(tab_expert[0:1, st.h, bass.ds(st.k, 1)], min_val=0, max_val=E - 1)
                if lead:
                    pe.wait_ge(we_lo, e * 2 + 2)
                pe.wait_ge(tokT_lo, st.count())
                if st.has(2):
                    pe.wait_ge(y_biased, st.count(2))
                product(y_bank(st.b2), [((tokT[:, st.b2, 0, k, :], tokT[:, st.b2, 1, k, :]),
                                         (we[:, 0, e, k, :], we[:, 1, e, k, :])) for k in range(KC)]).then_inc(y_mm, 1)

            lead = lead_steps()
            for c in range(C):
                turn_probs(T - 1, c)
                if c >= 1:
                    times_values(T - 1, c - 1)
                if c == 3:
                    turn_rows(T - 2)
                if c == 4:
                    gate_logits(T - 2)
            ranks(T - 2)
            turn_block(lead[0])
            times_values(T - 1, C - 1)
            pe.wait_ge(tables_done, 1)
            for i, st in enumerate(lead):
                turn_block((lead + turn_steps(0))[i + 1])
                multiply_block(st, True)
                if i == 1:
                    turn_rows(T - 1)
                if i == 2:
                    gate_logits(T - 1)
                if i == 3:
                    ranks(T - 1)
            pe.wait_ge(we_lo, 2 * E)
            pe.wait_ge(tables_done, 2)
            with pe.Fori(0, TURNS) as j:
                steps = turn_steps(j) + turn_steps(j + 1)[:1]
                for st, after in zip(steps, steps[1:]):
                    turn_block(after)
                    multiply_block(st, False)
            tail = tail_steps()
            for i, st in enumerate(tail):
                if i + 1 < LEAD:
                    turn_block(tail[i + 1])
                multiply_block(st, False)


def kernel(x, adj, L0_gnn_key, L0_gnn_value, L0_gnn_Wq, L0_gnn_bq, L0_gnn_Wk, L0_gnn_bk, L0_gnn_Wv, L0_gnn_bv,
           L0_gnn_Wm, L0_gnn_bm, L0_ffn_Wg, L0_ffn_bg, L0_ffn_We, L0_ffn_be):
    import numpy as np
    import concourse.bacc as bacc
    from concourse.bass_utils import run_bass_kernel_spmd

    nc = bacc.Bacc("TRN2", target_bir_lowering=False, num_devices=1)
    laid_out = {
        "x": x, "adj": adj,
        "keyT": np.asarray(L0_gnn_key).T, "valueT": np.asarray(L0_gnn_value).T,
        "Wq": L0_gnn_Wq, "bq": L0_gnn_bq, "Wk": L0_gnn_Wk, "bk": L0_gnn_bk, "Wv": L0_gnn_Wv, "bv": L0_gnn_bv,
        "WmT": np.asarray(L0_gnn_Wm).T, "bm": L0_gnn_bm,
        "Wg": L0_ffn_Wg, "bg": L0_ffn_bg,
        "WeT": np.asarray(L0_ffn_We).transpose(0, 2, 1), "be": L0_ffn_be,
    }
    arrays, args = {}, []
    for name, a in laid_out.items():
        a = np.ascontiguousarray(a)
        arrays[f"in_{name}"] = a
        args.append(nc.dram_tensor(f"in_{name}", a.shape, mybir.dt.from_np(a.dtype), kind="ExternalInput").ap())
    halves, rows = 2, x.shape[0] // 2
    results = [nc.dram_tensor(f"out_{h}", (rows + P, x.shape[1]), mybir.dt.float32, kind="ExternalOutput").ap()
               for h in range(halves)]
    graph_attention_moe_kernel(nc, *args, results)
    r = run_bass_kernel_spmd(nc, [arrays], core_ids=[0])
    return np.concatenate([r.results[0][f"out_{h}"][:rows] for h in range(halves)], axis=0)
```
